# Optimizing a Trainium2 kernel written in Bass

```python
import numpy as np
import jax
import jax.numpy as jnp

def _softmax(x, axis=-1):
    return jax.nn.softmax(x, axis=axis)

def _gelu(x):
    return jax.nn.gelu(x, approximate=True)

def _silu(x):
    return jax.nn.silu(x)

def _sigmoid(x):
    return jax.nn.sigmoid(x)

def _layernorm(x, axis=-1, eps=1e-05):
    m = jnp.mean(x, axis=axis, keepdims=True)
    v = jnp.var(x, axis=axis, keepdims=True)
    return (x - m) / jnp.sqrt(v + eps)

def _scatter_add(tgt, idx, src, axis=0):
    return tgt.at[idx].add(src)

def _segment_sum(src, seg, n):
    return jax.ops.segment_sum(src, seg, n)
kernel_name = 'mk_xattn_ffn_d1_seqx_r8_15c625'

def setup_inputs(seed: int=0):
    np.random.seed(seed)
    _w = jnp.asarray

    def _rec_inputs():
        import jax
        import jax.numpy as jnp
        _rk = jax.random.key(seed)
        x = -0.0002928 + 1 * jax.random.normal(jax.random.fold_in(_rk, 1), (64, 128, 128), jnp.float32)
        _lenS = 128 - jax.random.randint(jax.random.fold_in(_rk, 7), (64,), 0, max(1, 128 // 4) + 1, jnp.int32)
        _lenS2 = 120 - jax.random.randint(jax.random.fold_in(_rk, 8), (64,), 0, max(1, 120 // 4) + 1, jnp.int32)
        _ctx_1024P = jax.random.normal(jax.random.fold_in(_rk, 11), (64, 16, 128), jnp.float32)
        _ctx_1024c = jax.random.dirichlet(jax.random.fold_in(_rk, 511), 0.3 * jnp.ones((16,), jnp.float32), (64, 120))
        _ctx_1024t = jnp.einsum('bsk,bkd->bsd', _ctx_1024c, _ctx_1024P)
        _ctx_1024t = _ctx_1024t * jax.lax.rsqrt(jnp.mean(jnp.square(_ctx_1024t)) + 1e-12) * 0.953939
        ctx_1024 = -1.39393e-06 + 0.999914 * (_ctx_1024t + 0.3 * jax.random.normal(jax.random.fold_in(_rk, 611), (64, 120, 128), jnp.float32))
        _validS = jnp.arange(128)[None, :] < _lenS[:, None]
        _validS2 = jnp.arange(120)[None, :] < _lenS2[:, None]
        _causal = jnp.tril(jnp.ones((128, 128), dtype=bool))
        mask_BxS2_bf0 = jnp.logical_not(jnp.ones((64, 120), dtype=bool))
        return (x, ctx_1024, mask_BxS2_bf0)
    x, ctx_1024, mask_BxS2_bf0 = _rec_inputs()

    def _L0_xattn_setup():
        import jax, jax.numpy as jnp
        import numpy as np
        D_MODEL = 128
        N_HEADS = 16
        SEQ = 256
        BATCH = 2
        key = jax.random.key(seed)
        ks = jax.random.split(key, 12)
        s = 1.0 / np.sqrt(D_MODEL)
        return {'q_input': jax.random.normal(ks[0], (BATCH, SEQ, D_MODEL), jnp.float32), 'k_input': jax.random.normal(ks[1], (BATCH, SEQ, D_MODEL), jnp.float32), 'v_input': jax.random.normal(ks[2], (BATCH, SEQ, D_MODEL), jnp.float32), 'key_padding_mask': jnp.zeros((BATCH, SEQ), dtype=bool), 'wq': jax.random.normal(ks[3], (D_MODEL, D_MODEL), jnp.float32) * s, 'bq': jnp.zeros((D_MODEL,), jnp.float32), 'wk': jax.random.normal(ks[4], (D_MODEL, D_MODEL), jnp.float32) * s, 'bk': jnp.zeros((D_MODEL,), jnp.float32), 'wv': jax.random.normal(ks[5], (D_MODEL, D_MODEL), jnp.float32) * s, 'bv': jnp.zeros((D_MODEL,), jnp.float32), 'wo': jax.random.normal(ks[6], (D_MODEL, D_MODEL), jnp.float32) * s, 'bo': jnp.zeros((D_MODEL,), jnp.float32)}
    _L0_xattn_all = _L0_xattn_setup()
    _L0_xattn_in = {k: v for k, v in _L0_xattn_all.items() if k in ('wq', 'bq', 'wk', 'bk', 'wv', 'bv', 'wo', 'bo')}
    del _L0_xattn_all

    def _L0_ffn_setup():
        import jax, jax.numpy as jnp
        import numpy as np
        H = 128
        I = 4 * H
        E = 8
        K = 2
        B, S = (2, 128)
        STD = 0.02 / np.sqrt(H)
        key = jax.random.key(seed)
        ks = jax.random.split(key, 8)
        x = jax.random.normal(ks[0], (B, S, H), dtype=jnp.float32)
        gate_w = jax.random.normal(ks[1], (H, E), dtype=jnp.float32) * STD
        bias = jnp.zeros((E,), dtype=jnp.float32)
        up_w = jax.random.normal(ks[2], (E, H, I), dtype=jnp.float32) * STD
        up_b = jnp.zeros((E, I), dtype=jnp.float32)
        down_w = jax.random.normal(ks[3], (E, I, H), dtype=jnp.float32) * STD
        down_b = jnp.zeros((E, H), dtype=jnp.float32)
        sw_up = jax.random.normal(ks[4], (H, I), dtype=jnp.float32) * STD
        sb_up = jnp.zeros((I,), dtype=jnp.float32)
        sw_down = jax.random.normal(ks[5], (I, H), dtype=jnp.float32) * STD
        sb_down = jnp.zeros((H,), dtype=jnp.float32)
        return {'x': x, 'gate_w': gate_w, 'bias': bias, 'up_w': up_w, 'up_b': up_b, 'down_w': down_w, 'down_b': down_b, 'sw_up': sw_up, 'sb_up': sb_up, 'sw_down': sw_down, 'sb_down': sb_down}
    _L0_ffn_all = _L0_ffn_setup()
    _L0_ffn_in = {k: v for k, v in _L0_ffn_all.items() if k in ('gate_w', 'bias', 'up_w', 'up_b', 'down_w', 'down_b', 'sw_up', 'sb_up', 'sw_down', 'sb_down')}
    del _L0_ffn_all
    return {'x': x, 'ctx_1024': ctx_1024, 'mask_BxS2_bf0': mask_BxS2_bf0, 'L0_xattn_wq': _L0_xattn_in['wq'], 'L0_xattn_bq': _L0_xattn_in['bq'], 'L0_xattn_wk': _L0_xattn_in['wk'], 'L0_xattn_bk': _L0_xattn_in['bk'], 'L0_xattn_wv': _L0_xattn_in['wv'], 'L0_xattn_bv': _L0_xattn_in['bv'], 'L0_xattn_wo': _L0_xattn_in['wo'], 'L0_xattn_bo': _L0_xattn_in['bo'], 'L0_ffn_gate_w': _L0_ffn_in['gate_w'], 'L0_ffn_bias': _L0_ffn_in['bias'], 'L0_ffn_up_w': _L0_ffn_in['up_w'], 'L0_ffn_up_b': _L0_ffn_in['up_b'], 'L0_ffn_down_w': _L0_ffn_in['down_w'], 'L0_ffn_down_b': _L0_ffn_in['down_b'], 'L0_ffn_sw_up': _L0_ffn_in['sw_up'], 'L0_ffn_sb_up': _L0_ffn_in['sb_up'], 'L0_ffn_sw_down': _L0_ffn_in['sw_down'], 'L0_ffn_sb_down': _L0_ffn_in['sb_down']}

def reference(x, ctx_1024, mask_BxS2_bf0, L0_xattn_wq, L0_xattn_bq, L0_xattn_wk, L0_xattn_bk, L0_xattn_wv, L0_xattn_bv, L0_xattn_wo, L0_xattn_bo, L0_ffn_gate_w, L0_ffn_bias, L0_ffn_up_w, L0_ffn_up_b, L0_ffn_down_w, L0_ffn_down_b, L0_ffn_sw_up, L0_ffn_sb_up, L0_ffn_sw_down, L0_ffn_sb_down):
    import jax
    import jax.numpy as jnp

    def _L0_xattn_ref(q_input, k_input, v_input, key_padding_mask, wq, bq, wk, bk, wv, bv, wo, bo):
        import jax, jax.numpy as jnp
        import numpy as np
        D_MODEL = 128
        N_HEADS = 16
        SEQ = 256
        BATCH = 2
        B, Lq, _ = q_input.shape
        Lk = k_input.shape[1]
        d_head = D_MODEL // N_HEADS
        Q = q_input @ wq.T + bq
        K = k_input @ wk.T + bk
        V = v_input @ wv.T + bv
        Qh = Q.reshape(B, Lq, N_HEADS, d_head).transpose(0, 2, 1, 3)
        Kh = K.reshape(B, Lk, N_HEADS, d_head).transpose(0, 2, 1, 3)
        Vh = V.reshape(B, Lk, N_HEADS, d_head).transpose(0, 2, 1, 3)
        scores = jnp.einsum('bhqd,bhkd->bhqk', Qh, Kh) / jnp.sqrt(jnp.float32(d_head))
        causal = jnp.arange(Lk)[None, :] > jnp.arange(Lq)[:, None]
        scores = jnp.where(causal[None, None], -jnp.inf, scores)
        scores = jnp.where(key_padding_mask[:, None, None, :], -jnp.inf, scores)
        probs = jnp.where(jnp.all(jnp.isinf(scores)), jnp.full_like(scores, 1.0 / Lk), jax.nn.softmax(scores, axis=-1))
        out = jnp.einsum('bhqk,bhkd->bhqd', probs, Vh)
        out = out.transpose(0, 2, 1, 3).reshape(B, Lq, D_MODEL)
        return out @ wo.T + bo

    def _L0_ffn_ref(x, gate_w, bias, up_w, up_b, down_w, down_b, sw_up, sb_up, sw_down, sb_down):
        import jax, jax.numpy as jnp
        import numpy as np
        H = 128
        I = 4 * H
        E = 8
        K = 2
        B, S = (2, 128)
        STD = 0.02 / np.sqrt(H)
        b, s, h = x.shape
        xf = x.reshape(-1, h)
        T = xf.shape[0]
        scores = jax.nn.sigmoid(xf @ gate_w + bias)
        top_scores, top_idx = jax.lax.top_k(scores, K)
        top_scores = top_scores / (jnp.sum(top_scores, axis=-1, keepdims=True) + 1e-06)
        w = jnp.zeros((T, E), dtype=xf.dtype).at[jnp.arange(T)[:, None], top_idx].add(top_scores)
        up = jnp.einsum('th,ehi->tei', xf, up_w) + up_b
        hact = jax.nn.gelu(up, approximate=False)
        eo = jnp.einsum('tei,eih->teh', hact, down_w) + down_b
        combined = jnp.einsum('teh,te->th', eo * 0.1, w)
        shared = (jax.nn.gelu(xf @ sw_up + sb_up, approximate=False) @ sw_down + sb_down) * 0.1
        out = (shared + combined).reshape(b, s, h)
        out = out / (jnp.max(jnp.abs(out), axis=-1, keepdims=True) + 1e-06)
        return out
    x = x + _L0_xattn_ref(_layernorm(x, axis=-1), ctx_1024, ctx_1024, mask_BxS2_bf0, L0_xattn_wq, L0_xattn_bq, L0_xattn_wk, L0_xattn_bk, L0_xattn_wv, L0_xattn_bv, L0_xattn_wo, L0_xattn_bo)
    x = x + _L0_ffn_ref(_layernorm(x, axis=-1), L0_ffn_gate_w, L0_ffn_bias, L0_ffn_up_w, L0_ffn_up_b, L0_ffn_down_w, L0_ffn_down_b, L0_ffn_sw_up, L0_ffn_sb_up, L0_ffn_sw_down, L0_ffn_sb_down)
    return x

_drawn_inputs = setup_inputs


def setup_inputs(seed=0):
    import zlib

    import numpy as np

    out = dict(_drawn_inputs(seed))
    spreads = {'L0_xattn_bq': (0.0, 0.291),
     'L0_xattn_bk': (0.0, 0.8),
     'L0_xattn_bv': (0.0, 0.1),
     'L0_xattn_bo': (0.0, 0.1),
     'L0_ffn_bias': (0.0, 0.1),
     'L0_ffn_up_b': (0.0, 0.8),
     'L0_ffn_down_b': (0.0, 0.1),
     'L0_ffn_sb_up': (0.0, 0.8),
     'L0_ffn_sb_down': (0.0, 0.1)}
    factors = {'L0_ffn_up_w': 8.0, 'L0_ffn_down_w': 8.0, 'L0_ffn_sw_up': 8.0, 'L0_ffn_sw_down': 8.0}
    for name, (base, spread) in spreads.items():
        noise = np.random.default_rng([zlib.crc32(name.encode()), seed]).standard_normal(out[name].shape)
        drawn = base * np.exp(spread * noise) if base else spread * noise
        out[name] = jnp.asarray(drawn.astype(out[name].dtype))
    for name, factor in factors.items():
        out[name] = (out[name] * factor).astype(out[name].dtype)
    return out
```

```python
from contextlib import ExitStack

import numpy as np

import concourse.bass as bass
from concourse import mybir

F32 = mybir.dt.float32
F32R = mybir.dt.float32r
BF16 = mybir.dt.bfloat16
U8 = mybir.dt.uint8
I32 = mybir.dt.int32
ALU = mybir.AluOpType
ACT = mybir.ActivationFunctionType
AX = mybir.AxisListType

NB, LQ, LK, D = 64, 128, 120, 128
NE, FF = 8, 512
GB = 4
NG = NB // GB
T = GB * LQ
TK = GB * LK
BIG = float(2.0 ** 100)
EPS = 1e-5
SCALE = float(1.0 / np.sqrt(8.0))
EXPERTS = NE + 1
CH = EXPERTS * 4
START = 38

C_ID, C_CAUS, C_NMQ, C_NMK, C_KONE, C_PRIO, C_ONES, C_TRIL, C_N = 0, 128, 248, 249, 250, 251, 283, 411, 539


def constants():
    c = np.zeros((128, C_N), np.float32)
    c[:, C_ID:C_ID + 128] = np.eye(128)
    q, k = np.arange(128)[:, None], np.arange(LK)[None, :]
    c[:, C_CAUS:C_CAUS + LK] = np.where(k > q, -BIG, 0.0)
    row = np.arange(128)
    part, dd = row % 32 // 8, row % 8
    c[:, C_NMQ] = np.where(part == 2, -1.0, 0.0)
    c[:, C_NMK] = np.where(part == 1, -1.0, 0.0)
    c[:, C_KONE] = np.where((part == 3) & (dd < 2), 1.0, 0.0)
    c[:, C_PRIO:C_PRIO + 32] = np.tile(8.0 - np.arange(8), 4)
    j = np.arange(4)[:, None]
    m = np.arange(32)[None, :]
    c[:, C_ONES:C_ONES + 128] = (m // 8 == j).astype(np.float32).reshape(-1)
    kk, qq = np.arange(128)[:, None], np.arange(128)[None, :]
    c[:, C_TRIL:C_TRIL + 128] = (kk <= qq)
    return c


class Queues:

    def __init__(self, sem):
        self.sem, self.sems, self.count = sem, {}, {}
        self.ops = {n: [] for n in ("tensor", "vector", "scalar", "gpsimd", "sync")}

    def add(self, engine, fn, wait=(), sig=None, by=1):
        token = None
        if sig is not None:
            if sig not in self.sems:
                self.sems[sig], self.count[sig] = self.sem(sig), 0
            self.count[sig] += by
            token = (sig, self.count[sig])
        self.ops[engine].append((fn, [w for w in wait if w is not None], sig, by))
        return token

    def play(self, engine, eng):
        seen = {}
        for fn, wait, sig, by in self.ops[engine]:
            for name, value in wait:
                if seen.get(name, 0) < value:
                    eng.wait_ge(self.sems[name], value)
                    seen[name] = value
            ins = fn(eng)
            if sig is not None:
                ins.then_inc(self.sems[sig], by)


def xattn_moe_kernel(nc, x, ctxT, mask, maskT, wqT, wkT, wvT, woT, bqT, bkT, bv, bo, gate_w, gbias,
                     up_w, up_bT, down_w, down_bT, sw_up, sb_upT, sw_down, sb_downT, consts, out):
    w_dram = nc.dram_tensor("w_scratch", (2, 32, 128), F32, kind="Internal").ap()
    with ExitStack() as ctx:
        def sb(name, shape, dt=F32):
            return ctx.enter_context(nc.sbuf_tensor(name, shape, dt))

        Q = Queues(lambda n: ctx.enter_context(nc.semaphore(n)))

        def pe(fn, wait=(), sig=None):
            return Q.add("tensor", fn, wait, sig)

        def dve(fn, wait=(), sig=None):
            return Q.add("vector", fn, wait, sig)

        def act(fn, wait=(), sig=None):
            return Q.add("scalar", fn, wait, sig)

        def pool(fn, wait=(), sig=None):
            return Q.add("gpsimd", fn, wait, sig)

        def dma(dst, src, wait=(), sig=None, queue="sync"):
            return Q.add(queue, lambda e: e.dma_start(dst, src), wait, sig, 16)

        banks = [ctx.enter_context(nc.psum_tensor(f"bank{i}", [128, 512], F32)) for i in range(8)]
        UPB, DNB, ATT = banks[0:2], banks[2:4], banks[4:8]

        con = sb("con", [128, C_N])
        ident = con[:, C_ID:C_ID + 128]
        identb = sb("identb", [128, 128], BF16)
        trilb = sb("trilb", [128, 128], BF16)
        onesb = sb("onesb", [128, 128], BF16)
        vis = sb("vis", [128, 64], BF16)
        visi = sb("visi", [128, 16], I32)
        visu = visi[:, :].bitcast(U8)
        poison = sb("poison", [128, 64])
        pz = sb("pz", [128, 64])
        pt_ = sb("pt_", [128, 2])
        nhalf = sb("nhalf", [128, 4])

        uph = sb("uph", [128, EXPERTS, FF], F32R)
        upl = sb("upl", [128, EXPERTS, FF], F32R)
        dnh = sb("dnh", [128, EXPERTS, 4, 128], F32R)
        dnl = sb("dnl", [128, EXPERTS, 4, 128], F32R)
        upb = sb("upb", [128, EXPERTS, 4])
        dnb = sb("dnb", [128, EXPERTS])
        wqh = sb("wqh", [128, 16, 4, 8], F32R)
        wql = sb("wql", [128, 16, 4, 8], F32R)
        wkh = sb("wkh", [128, 16, 4, 8], F32R)
        wkl = sb("wkl", [128, 16, 4, 8], F32R)
        wv = sb("wv", [128, 128])
        wo = sb("wo", [128, 128])
        bqr = sb("bqr", [128, 4])
        bkr = sb("bkr", [128, 4])
        bvb = sb("bvb", [128, 128])
        bob = sb("bob", [128, 128])
        gwf = sb("gwf", [128, 8])
        gwh = sb("gwh", [128, 8], F32R)
        gwl = sb("gwl", [128, 8], F32R)
        gb = sb("gb", [8, 1])
        ngb = sb("ngb", [8, 1])

        xs_ = [sb(f"x{i}", [128, GB, 128]) for i in range(2)]
        x1_ = [sb(f"x1_{i}", [128, GB, 128]) for i in range(2)]
        xhat = sb("xhat", [128, GB, 128])
        xth = sb("xth", [128, T], F32R)
        xtl = sb("xtl", [128, T], F32R)
        fth_ = [sb(f"fth{i}", [128, T], F32R) for i in range(2)]
        ftl_ = [sb(f"ftl{i}", [128, T], F32R) for i in range(2)]
        cxf = sb("cxf", [128, TK])
        cxh = sb("cxh", [128, TK], F32R)
        cxl = sb("cxl", [128, TK], F32R)
        st = sb("st", [128, GB, 6])
        mv = sb("mv", [128, GB, 2])
        ve = sb("ve", [128, GB])
        rstd = sb("rstd", [128, GB])
        st2 = sb("st2", [128, GB, 6])
        mv2 = sb("mv2", [128, GB, 2])
        ve2 = sb("ve2", [128, GB])
        rstd2 = sb("rstd2", [128, GB])
        keyb = [sb(f"keyb{i}", [128, GB, LK // 4], I32) for i in range(2)]
        maskb = sb("maskb", [128, GB, LK], BF16)
        px = sb("px", [128, T])
        pr = sb("pr", [128, T], F32R)
        qst = sb("qst", [128, 4, T], F32R)
        kst = sb("kst", [128, 4, TK], F32R)
        kblk = sb("kblk", [128, 4, 4, LK], F32R)
        qblk_ = [sb(f"qblk{i}", [128, 4, 4, 128], F32R) for i in range(2)]
        NP = 5
        prob = [sb(f"prob{i}", [128, 512]) for i in range(NP)]
        vm_ = [sb(f"vm{i}", [128, 16, 32]) for i in range(2)]
        nm = sb("nm", [128, 16])
        nmh = sb("nmh", [128, 16], F32R)
        nm2 = sb("nm2", [128, 16, 2])
        nmt = sb("nmt", [8, 4, 128], F32R)
        rsum = sb("rsum", [128, 128])
        oT = sb("oT", [128, 128])
        er = sb("er", [8, T])
        s1 = sb("s1", [128, 4, 8])
        s2 = sb("s2", [128, 4, 8])
        eq = sb("eq", [128, 4, 8])
        oh1 = sb("oh1", [128, 4, 8])
        oh2 = sb("oh2", [128, 4, 8])
        m1 = sb("m1", [128, 4])
        m2 = sb("m2", [128, 4])
        pm = sb("pm", [128, 4])
        wgt = sb("wgt", [128, 4, 8])
        wts = sb("wts", [32, 128])
        NW = 3
        wb_ = [sb(f"wb{i}", [128, T]) for i in range(NW)]
        gf_ = [sb(f"gf{i}", [128, T]) for i in range(2)]
        gh_ = [sb(f"gh{i}", [128, T], F32R) for i in range(3)]
        gl_ = [sb(f"gl{i}", [128, T], F32R) for i in range(3)]
        eo_ = [sb(f"eo{i}", [128, T]) for i in range(2)]
        acc = sb("acc", [128, T])
        am = sb("am", [128, 4])
        ar = sb("ar", [128, 4])

        def f(ap):
            return ap.bitcast(F32)

        spare = [(i, None) for i in range(len(ATT))]

        def bank():
            i, last_read = spare.pop(0)
            return i, ATT[i], last_read

        def give(i, last_read):
            spare.append((i, last_read))

        t_con = dma(con[:, :], consts, sig="d_con")
        for dst, src in ((wv[:, :], wvT), (wo[:, :], woT), (gwf[:, :], gate_w), (gb[:, :], gbias),
                         (bvb[:, :], bv.partition_broadcast(128)), (bob[:, :], bo.partition_broadcast(128)),
                         (xhat[:, 0, :], wqT), (xhat[:, 1, :], wkT)):
            t_small = dma(dst, src, sig="d_small")
        t_bz = pool(lambda e: e.memset(bqr[:, :], 0.0), sig="p_bz")
        t_bz = pool(lambda e: e.memset(bkr[:, :], 0.0), sig="p_bz")
        for j in range(4):
            for part in range(3):
                r = 32 * j + 8 * part
                t_bias = dma(bqr[r:r + 8, :], bqT[8 * j:8 * j + 8, :], wait=[t_bz], sig="d_bias")
                t_bias = dma(bkr[r:r + 8, :], bkT[8 * j:8 * j + 8, :], wait=[t_bz], sig="d_bias")

        t_load = {}

        def load(n):
            p = n % 2
            prev = t_free_x.get(n - 2)
            dma(xs_[p][:, :, :], x[GB * n:GB * n + GB].rearrange("b q d -> q b d"), wait=[prev], sig=f"d_x{p}")
            t_load[n] = dma(keyb[p][:, :, :], mask[GB * n:GB * n + GB, :].partition_broadcast(128),
                            wait=[t_mask.get(n - 2)], sig=f"d_x{p}")

        def load_ctx(n):
            t_ctx[n] = dma(cxf[:, :], ctxT[:, TK * n:TK * n + TK], wait=[t_cxl.get(n - 1)], sig="d_ctx")

        t_free_x, t_mask, t_ctx, t_cxl = {}, {}, {}, {}
        load(0)
        load_ctx(0)
        t_vis = dma(visi[0:LK, :], maskT, sig="d_vis")
        t_ub = dma(upb[:, 0, :], sb_upT, sig="d_fb")
        t_ub = dma(upb[:, 1:, :], up_bT.rearrange("p (e c) -> p e c", e=8), sig="d_fb")
        t_ub = dma(dnb[:, 0:1], sb_downT, sig="d_fb")
        t_ub = dma(dnb[:, 1:], down_bT, sig="d_fb")

        t_nh = pool(lambda e: e.memset(nhalf[:, :], -0.5), sig="p_nh")
        t_z = pool(lambda e: e.memset(f(kblk[:, :, :, :]), 0.0), sig="p_zk")
        t_zq = None
        for qb in qblk_:
            t_zq = pool(lambda e, qb=qb: e.memset(f(qb[:, :, :, :]), 0.0), sig="p_zq")
        for w in (wqh, wql, wkh, wkl):
            t_zw = pool(lambda e, w=w: e.memset(f(w[:, :, :, :]), 0.0), sig="p_zw")
        for v in vm_:
            t_zv = pool(lambda e, v=v: e.memset(v[:, :, :], 0.0), sig="p_zv")
        t_one = pool(lambda e: e.memset(onesb[:, :], 1.0), sig="p_one")

        for src, wh, wl in ((0, wqh, wql), (1, wkh, wkl)):
            raw = xhat[:, src, :].rearrange("p (h o d) -> p h o d", h=16, o=1).to_broadcast([128, 16, 3, 8])
            t = dve(lambda e, wh=wh, raw=raw: e.tensor_copy(wh[:, :, 0:3, :], raw), wait=[t_small, t_zw], sig="v_wh")
            t_w = dve(lambda e, wh=wh, wl=wl, raw=raw: e.tensor_tensor(
                wl[:, :, 0:3, :], raw, f(wh[:, :, 0:3, :]), ALU.subtract), wait=[t], sig="v_wl")
        t = dve(lambda e: e.tensor_copy(gwh[:, :], gwf[:, :]), sig="v_gw")
        dve(lambda e: e.tensor_tensor(gwl[:, :], gwf[:, :], f(gwh[:, :]), ALU.subtract), wait=[t], sig="v_gw")
        t_gw = dve(lambda e: e.tensor_scalar(ngb[:, :], gb[:, :], -1.0, None, ALU.mult), sig="v_gw")
        dve(lambda e: e.tensor_copy(identb[:, :], ident), wait=[t_con], sig="v_id")
        t_id = dve(lambda e: e.tensor_copy(trilb[:, :], con[:, C_TRIL:C_TRIL + 128]), sig="v_id")
        t_bk = dve(lambda e: e.tensor_scalar(bkr[:, :], bkr[:, :], con[:, C_KONE:C_KONE + 1], None, ALU.add),
                   wait=[t_bias], sig="v_bk")

        t = dve(lambda e: e.tensor_scalar(vis[0:LK, :], visu[0:LK, :], -1.0, 1.0, ALU.mult, ALU.add),
                wait=[t_vis], sig="v_vis")
        i, bk, free = bank()
        pe(lambda e, bk=bk: e.matmul(bk[:, 0:64], trilb[0:LK, :], vis[0:LK, :], start=True, stop=True),
           wait=[t, t_id, t_one])
        t = pe(lambda e, bk=bk: e.matmul(bk[:, 64:128], onesb[0:LK, :], vis[0:LK, :], start=True, stop=True,
                                         skip_group_check=True), sig="m_vis")
        dve(lambda e, bk=bk: e.tensor_reduce(pt_[:, 0:1], bk[:, 64:128], AX.X, ALU.add), wait=[t], sig="v_poi")
        t = dve(lambda e, bk=bk: e.tensor_scalar(pz[:, :], bk[:, 0:64], 0.0, 3e38, ALU.is_equal, ALU.mult), sig="v_poi")
        give(i, t)
        t = dve(lambda e: e.tensor_scalar(pt_[:, 1:2], pt_[:, 0:1], 0.0, None, ALU.is_gt), wait=[t], sig="v_poi")
        t = dve(lambda e: e.tensor_scalar(poison[:, :], pz[:, :], pt_[:, 1:2], 10.0, ALU.mult, ALU.mult),
                wait=[t], sig="v_poi")
        t_poison = dve(lambda e: e.tensor_tensor(pz[:, :], poison[:, :], poison[:, :], ALU.subtract),
                       wait=[t], sig="v_poi")

        stage_free = [None] * NP
        t_fw = {}
        k = 0
        for ex in range(EXPERTS):
            for what in range(2):
                s = prob[k % NP]
                if what == 0:
                    src = sw_up if ex == 0 else up_w[ex - 1]
                    dst = s[:, :]
                    h, l = uph[:, ex, :], upl[:, ex, :]
                else:
                    src = (sw_down if ex == 0 else down_w[ex - 1]).rearrange("(c p) h -> p c h", p=128)
                    dst = s[:, :].rearrange("p (c h) -> p c h", c=4)
                    h = dnh[:, ex, :, :].rearrange("p c h -> p (c h)")
                    l = dnl[:, ex, :, :].rearrange("p c h -> p (c h)")
                td = dma(dst, src, wait=[stage_free[k % NP]], sig=f"d_w{k % NP}")
                ta = act(lambda e, h=h, s=s: e.activation(h, s[:, :], ACT.Copy), wait=[td], sig="a_wh")
                tp = pool(lambda e, h=h, l=l, s=s: e.tensor_tensor(l, s[:, :], f(h), ALU.subtract),
                          wait=[ta, td], sig="p_wl")
                stage_free[k % NP] = tp
                t_fw[ex] = tp
                k += 1
        for i in range(NP):
            t_zp = pool(lambda e, i=i: e.memset(prob[i][:, :], 0.0), wait=[stage_free[i]], sig="p_zp")

        S = {}

        def ln_a(n, src, stats, agg, v, wait, tag):
            for b in range(GB):
                t = dve(lambda e, b=b: e.bn_stats(stats[:, b, :], src[:, b, :]), wait=wait, sig=f"v_st{tag}")
            for b in range(GB):
                t = dve(lambda e, b=b: e.bn_aggr(agg[:, b, :], stats[:, b, :]), wait=[t], sig=f"v_ag{tag}")
            return dve(lambda e: e.tensor_scalar(v[:, :], agg[:, :, 1], EPS, None, ALU.add),
                       wait=[t], sig=f"v_ve{tag}")

        def a_ln(n):
            xt = xs_[n % 2]
            t = ln_a(n, xt, st, mv, ve, [t_load[n], t_w], "1")
            S["rs", n] = pool(lambda e: e.tensor_tensor(rstd[:, :], ve[:, :], nhalf[:, :], ALU.pow),
                              wait=[t, t_nh, S.get(("xhat", n - 1))], sig="p_rs1")
            S["msk", n] = dve(lambda e: e.scalar_tensor_tensor(
                out=maskb[:, :, :], in0=keyb[n % 2][:, :, :].bitcast(U8), scalar=-BIG,
                in1=con[:, C_CAUS:C_CAUS + LK].unsqueeze(1).to_broadcast([128, GB, LK]),
                op0=ALU.mult, op1=ALU.min), wait=[t_con, S.get(("Bd", n - 1, 3))], sig="v_msk")
            t_mask[n] = S["msk", n]

        def a_ctx(n):
            t = dve(lambda e: e.tensor_copy(cxh[:, :], cxf[:, :]), wait=[t_ctx[n], S.get(("V", n - 1, 3))], sig="v_ch")
            S["ch", n] = t
            S["cx", n] = dve(lambda e: e.tensor_tensor(cxl[:, :], cxf[:, :], f(cxh[:, :]), ALU.subtract),
                             wait=[t], sig="v_cl")
            t_cxl[n] = S["cx", n]

        def a_xhat(n):
            xt = xs_[n % 2]
            for b in range(GB):
                t = dve(lambda e, b=b: e.tensor_scalar(
                    xhat[:, b, :], xt[:, b, :], mv[:, b, 0:1], rstd[:, b:b + 1], ALU.subtract, ALU.mult),
                    wait=[S["rs", n], S.get(("xt2", n - 1))], sig="v_xh")
            S["xhat", n] = t
            S["xb", n] = pool(lambda e: e.tensor_tensor(
                xt[:, :, :], xt[:, :, :], bob[:, :].unsqueeze(1).to_broadcast([128, GB, 128]), ALU.add),
                wait=[t, t_small], sig="p_xb")

        def tr4(src, wait, sig):
            i, bk, free = bank()
            for b in range(GB):
                t = pe(lambda e, b=b: e.transpose(bk[:, 128 * b:128 * b + 128], src[:, b, :], ident),
                       wait=[*wait, free], sig=sig)
            return i, bk, t

        def split(n, i, bk, t, hi, lo, wait, tag):
            th = act(lambda e: e.activation(hi[:, :], bk[:, :], ACT.Copy), wait=[t, *wait], sig=f"a_{tag}")
            tl = dve(lambda e: e.tensor_tensor(lo[:, :], bk[:, :], f(hi[:, :]), ALU.subtract),
                     wait=[th, *wait], sig=f"v_{tag}")
            give(i, tl)
            return tl

        def a_xT(n):
            S["xT", n] = i, bk, t = tr4(xhat, [S["xhat", n], t_con], "m_xT")
            S["xt1", n] = t

        def a_xTs(n):
            i, bk, t = S["xT", n]
            S["xt", n] = split(n, i, bk, t, xth, xtl, [S.get(("Qp", n - 1))], "xt")

        def project(n, g, wh, wl, ch, cl, N, wait, bias, nmc, dst, tag):
            i, bk, free = bank()
            cols = lambda w: w[:, 4 * g:4 * g + 4, :, :].rearrange("p a b c -> p (a b c)")
            pe(lambda e: e.matmul(bk[:, 0:N], cols(wh), ch[:, :], start=True, stop=False), wait=[*wait, t_w, free])
            pe(lambda e: e.matmul(bk[:, 0:N], cols(wh), cl[:, :], start=False, stop=False))
            t = pe(lambda e: e.matmul(bk[:, 0:N], cols(wl), ch[:, :], start=False, stop=True), sig=f"m_{tag}")
            ta = act(lambda e: e.activation(px[:, 0:N], bk[:, 0:N], ACT.Identity, bias=bias[:, g:g + 1]),
                     wait=[t, t_bk, t_bias, S.get("px")], sig=f"a_{tag}")
            give(i, ta)
            tr = dve(lambda e: e.tensor_copy(pr[:, 0:N], px[:, 0:N]), wait=[ta, S.get("px")], sig=f"v_{tag}r")
            S["px"] = dve(lambda e: e.scalar_tensor_tensor(
                out=dst[:, g, :], in0=f(pr[:, 0:N]), scalar=con[:, nmc:nmc + 1], in1=px[:, 0:N],
                op0=ALU.mult, op1=ALU.add), wait=[tr, t_con, S.get((tag + "free", n - 1))], sig=f"v_{tag}y")
            return t, S["px"]

        def a_k(n, g):
            _, S["Ks", n] = project(n, g, wkh, wkl, cxh, cxl, TK, [S["cx", n]], bkr, C_NMK, kst, "K")

        def a_q(n, g):
            S["Qp", n], S["Qs", n] = project(n, g, wqh, wql, xth, xtl, T, [S["xt", n]], bqr, C_NMQ, qst, "Q")

        def a_kblk(n, b):
            t = None
            for j in range(4):
                t = dma(f(kblk[32 * j:32 * j + 32, :, j, :]), f(kst[32 * j:32 * j + 32, :, LK * b:LK * b + LK]),
                        wait=[S["Ks", n], S.get(("Ad", prev(n, b))), t_z], sig="d_kb")
            S["kb", n, b] = t

        def prev(n, b, back=1):
            return GB * n + b - back

        def a_qblk(n, b):
            q = (GB * n + b) % 2
            for j in range(4):
                t = dma(f(qblk_[q][32 * j:32 * j + 24, :, j, :]), f(qst[32 * j:32 * j + 24, :, 128 * b:128 * b + 128]),
                        wait=[S["Qs", n], S.get(("Bdone", prev(n, b, 2))), t_zq], sig=f"d_qb{q}")

        def a_A(n, b, g):
            i, bk, free = bank()
            pe(lambda e: e.matmul(bk[:, 0:480], qst[:, g, 128 * b:128 * b + 128],
                                  kblk[:, g, :, :].rearrange("p a b -> p (a b)"), start=True, stop=False),
               wait=[S["kb", n, b], S["Qs", n], free])
            t = pe(lambda e: e.matmul(bk[:, 0:480].rearrange("p (j k) -> p j k", j=4), identb[:, :],
                                      maskb[:, b, :].unsqueeze(1).to_broadcast([128, 4, LK]), start=False, stop=True),
                   wait=[S["msk", n], t_id], sig="m_A")
            tm = dve(lambda e: e.tensor_reduce(nm[:, 4 * g:4 * g + 4], bk[:, 0:480].rearrange("p (j k) -> p j k", j=4),
                                               AX.X, ALU.max, negate=True),
                     wait=[t, S.get("nm_free")], sig="v_mx")
            give(i, tm)
            S["mx", n, b] = tm
            S["Ad", GB * n + b] = t
            if b == 3:
                S["Qfree", n] = t

        def a_nm(n, b):
            t = dve(lambda e: e.tensor_copy(nmh[:, :], nm[:, :]), wait=[S["mx", n, b]], sig="v_nm")
            dve(lambda e: e.tensor_copy(nm2[:, :, 0], f(nmh[:, :])), wait=[t, S.get("nmT_read")], sig="v_nm")
            S["nm", n, b] = dve(lambda e: e.tensor_tensor(nm2[:, :, 1], nm[:, :], f(nmh[:, :]), ALU.subtract),
                                wait=[t, S.get("nmT_read")], sig="v_nm")
            S["nm_free"] = S["nm", n, b]

        def a_nmT(n, b):
            i, bk, free = bank()
            for g in range(4):
                t = pe(lambda e, g=g: e.transpose(bk[0:8, 128 * g:128 * g + 128],
                                                  nm2[:, 4 * g:4 * g + 4, :].rearrange("p a b -> p (a b)"), ident),
                       wait=[S["nm", n, b], free], sig="m_nT")
            S["nmT_read"] = t
            S["nmT", n, b] = i, bk, t

        def a_nmTe(n, b):
            i, bk, t = S["nmT", n, b]
            te = dve(lambda e: e.tensor_copy(nmt[:, :, :], bk[0:8, :].rearrange("p (g q) -> p g q", g=4)),
                     wait=[t, S.get("nmt_free")], sig="v_nT")
            give(i, te)
            q = (GB * n + b) % 2
            for j in range(4):
                t = dma(f(qblk_[q][32 * j + 24:32 * j + 26, :, j, :]), f(nmt[2 * j:2 * j + 2, :, :]),
                        wait=[te, S.get(("Bdone", prev(n, b, 2))), t_zq], sig=f"d_qb{q}")
            S["qb", n, b] = t
            S["nmt_free"] = t

        def a_V(n, b):
            i, bk, free = bank()
            p = (GB * n + b) % 2
            cs = cxf_T(n, b)
            pe(lambda e: e.matmul(bk[0:LK, 0:128], cs[0], wv[:, :], start=True, stop=False),
               wait=[S["cx", n], t_small, free])
            t = pe(lambda e: e.matmul(bk[0:LK, 0:128], cs[1], wv[:, :], start=False, stop=True), sig="m_V")
            S["V", n, b] = t
            vm = vm_[p]
            free_v = S.get(("PVd", prev(n, b, 2)))
            for j in range(4):
                te = dve(lambda e, j=j: e.tensor_tensor(
                    vm[0:LK, :, :].rearrange("p (g j) m -> p g j m", g=4)[:, :, j, 8 * j:8 * j + 8],
                    bk[0:LK, 0:128].rearrange("p (g j d) -> p g j d", g=4, j=4)[:, :, j, :],
                    bvb[0:LK, :].rearrange("p (g j d) -> p g j d", g=4, j=4)[:, :, j, :], ALU.add),
                    wait=[t, t_small, t_zv, free_v], sig="v_V")
            give(i, te)
            S["vm", n, b] = te

        def cxf_T(n, b):
            return f(cxh[:, LK * b:LK * b + LK]), f(cxl[:, LK * b:LK * b + LK])

        def a_B(n, b, g):
            i, bk, free = bank()
            q = (GB * n + b) % 2
            s = (4 * (GB * n + b) + g) % NP
            pe(lambda e: e.matmul(bk[0:LK, :], kst[:, g, LK * b:LK * b + LK],
                                  qblk_[q][:, g, :, :].rearrange("p a b -> p (a b)"), start=True, stop=False),
               wait=[S["qb", n, b], free])
            t = pe(lambda e: e.matmul(bk[0:LK, :].rearrange("p (j k) -> p j k", j=4), maskb[:, b, :],
                                      identb[:, :].unsqueeze(1).to_broadcast([128, 4, 128]), start=False, stop=True),
                   sig="m_B")
            S["Bdone", GB * n + b] = t
            S["Bd", n, b] = t
            if b == 3:
                S["Kfree", n] = t
            te = act(lambda e: e.activation(prob[s][0:LK, :], bk[0:LK, :], ACT.Exp, scale=SCALE),
                     wait=[t, S.get(("pfree", s)), t_zp], sig="a_ex")
            give(i, te)
            S["P", n, b, g] = te

        ones32 = con[:, C_ONES:C_ONES + 128].rearrange("p (j m) -> p j m", j=4)

        def a_PV(n, b):
            i, bk, free = bank()
            vm = vm_[(GB * n + b) % 2]
            for half in range(2):
                for j in range(4):
                    for g in range(4):
                        s = (4 * (GB * n + b) + g) % NP
                        w = vm[:, 4 * g + j, :] if half == 0 else ones32[:, j, :]
                        t = pe(lambda e, g=g, j=j, s=s, w=w, half=half: e.matmul(
                            bk[32 * g:32 * g + 32, 128 * half:128 * half + 128], w,
                            prob[s][:, 128 * j:128 * j + 128], start=(j == 0), stop=(j == 3), skip_group_check=True),
                            wait=[S["P", n, b, g], S["vm", n, b], free, t_zp],
                            sig="m_PV")
                        if half == 1 and j == 3:
                            S["pfree", s] = t
            S["PVd", GB * n + b] = t
            S["PV", n, b] = i, bk, t

        def a_norm(n, b):
            i, bk, t = S["PV", n, b]
            tr = dve(lambda e: e.reciprocal(rsum[:, :], bk[:, 128:256]), wait=[t, S.get("oT")], sig="v_rs")
            to = dve(lambda e: e.tensor_tensor(oT[:, :], bk[:, 0:128], rsum[:, :], ALU.mult),
                     wait=[tr, S.get("Wo")], sig="v_oT")
            give(i, to)
            S["oT"] = to

        def a_wo(n, b):
            i, bk, free = bank()
            t = pe(lambda e: e.matmul(bk[:, 0:128], oT[:, :], wo[:, :], start=True, stop=True),
                   wait=[S["oT"], t_small, free], sig="m_wo")
            S["Wo"] = t
            S["wo", n, b] = i, bk, t

        def a_x1(n, b):
            i, bk, t = S["wo", n, b]
            xt, x1 = xs_[n % 2], x1_[n % 2]
            t = dve(lambda e: e.scalar_tensor_tensor(
                out=x1[:, b, :], in0=bk[:, 0:128], scalar=pz[:, GB * n + b:GB * n + b + 1], in1=xt[:, b, :],
                op0=ALU.add, op1=ALU.add), wait=[t, S["xb", n], t_poison, S.get(("outd", n - 2))], sig="v_x1")
            give(i, t)
            S["x1", n] = t
            if b == 3:
                t_free_x[n] = t

        def a_ln2(n):
            t = ln_a(n, x1_[n % 2], st2, mv2, ve2, [S["x1", n]], "2")
            S["rs2", n] = pool(lambda e: e.tensor_tensor(rstd2[:, :], ve2[:, :], nhalf[:, :], ALU.pow),
                               wait=[t, S.get(("xh2", n - 1))], sig="p_rs2")

        def a_xn2(n):
            x1 = x1_[n % 2]
            for b in range(GB):
                t = dve(lambda e, b=b: e.tensor_scalar(
                    xhat[:, b, :], x1[:, b, :], mv2[:, b, 0:1], rstd2[:, b:b + 1], ALU.subtract, ALU.mult),
                    wait=[S["rs2", n], S["xt1", n]], sig="v_xh2")
            S["xh2", n] = t

        def a_x2T(n):
            S["x2T", n] = i, bk, t = tr4(xhat, [S["xh2", n]], "m_x2T")
            S["xt2", n] = t

        def a_x2Ts(n):
            i, bk, t = S["x2T", n]
            S["ft", n] = split(n, i, bk, t, fth_[n % 2], ftl_[n % 2],
                               [S.get(("upd", n - 2)), S.get(("rt", n - 2))], "ft")

        def a_router(n):
            i, bk, free = bank()
            h, l = fth_[n % 2], ftl_[n % 2]
            pe(lambda e: e.matmul(bk[0:8, :], gwh[:, :], h[:, :], start=True, stop=False),
               wait=[S["ft", n], t_gw, free])
            pe(lambda e: e.matmul(bk[0:8, :], gwl[:, :], h[:, :], start=False, stop=False))
            t = pe(lambda e: e.matmul(bk[0:8, :], gwh[:, :], l[:, :], start=False, stop=True), sig="m_rt")
            S["rt", n] = t
            S["er", n] = act(lambda e: e.activation(er[:, :], bk[0:8, :], ACT.Exp, scale=-1.0, bias=ngb[:, 0:1]),
                             wait=[t, t_gw, S.get(("erT", n - 1))], sig="a_er")
            give(i, S["er", n])

        def a_erT(n):
            i, bk, free = bank()
            for b in range(GB):
                t = pe(lambda e, b=b: e.transpose(bk[:, 8 * b:8 * b + 8], er[:, 128 * b:128 * b + 128], ident[0:8, 0:8]),
                       wait=[S["er", n], free], sig="m_eT")
            S["erT", n] = t
            t = dve(lambda e: e.tensor_scalar(s2[:, :, :], bk[:, 0:32].rearrange("p (b e) -> p b e", b=4), 1.0, None,
                                              ALU.add), wait=[t], sig="v_top")
            give(i, t)
            S["top"] = dve(lambda e: e.reciprocal(s1[:, :, :], s2[:, :, :]), wait=[t], sig="v_top")

        prio = con[:, C_PRIO:C_PRIO + 32].rearrange("p (b e) -> p b e", b=4)

        def bc(a):
            return a[:, :].unsqueeze(2).to_broadcast([128, 4, 8])

        def first(src, m, oh):
            def step(fn):
                S["top"] = dve(fn, wait=[S["top"]], sig="v_top")
            step(lambda e: e.tensor_reduce(m[:, :], src[:, :, :], AX.X, ALU.max))
            step(lambda e: e.tensor_tensor(eq[:, :, :], src[:, :, :], bc(m), ALU.is_equal))
            step(lambda e: e.tensor_tensor(eq[:, :, :], eq[:, :, :], prio, ALU.mult))
            step(lambda e: e.tensor_reduce(pm[:, :], eq[:, :, :], AX.X, ALU.max))
            step(lambda e: e.tensor_tensor(oh[:, :, :], eq[:, :, :], bc(pm), ALU.is_equal))

        def a_top1(n):
            first(s1, m1, oh1)
            S["top"] = dve(lambda e: e.scalar_tensor_tensor(
                out=s2[:, :, :], in0=oh1[:, :, :], scalar=-4.0, in1=s1[:, :, :], op0=ALU.mult, op1=ALU.add),
                wait=[S["top"]], sig="v_top")

        def a_top2(n):
            first(s2, m2, oh2)

            def step(fn, wait=()):
                S["top"] = dve(fn, wait=[S["top"], *wait], sig="v_top")
            step(lambda e: e.tensor_tensor(oh1[:, :, :], oh1[:, :, :], oh2[:, :, :], ALU.add))
            step(lambda e: e.tensor_tensor(s1[:, :, :], s1[:, :, :], oh1[:, :, :], ALU.mult))
            step(lambda e: e.scalar_tensor_tensor(out=m1[:, :], in0=m1[:, :], scalar=1e-6, in1=m2[:, :],
                                                  op0=ALU.add, op1=ALU.add))
            step(lambda e: e.reciprocal(m2[:, :], m1[:, :]))
            step(lambda e: e.scalar_tensor_tensor(out=wgt[:, :, :], in0=s1[:, :, :], scalar=0.1, in1=bc(m2),
                                                  op0=ALU.mult, op1=ALU.mult), wait=[S.get("wT")])

        def a_wT(n):
            i, bk, free = bank()
            S["wT"] = t = pe(lambda e: e.transpose(bk[0:32, 0:128], wgt[:, :, :].rearrange("p b e -> p (b e)"), ident),
                             wait=[S["top"], free], sig="m_wT")
            t = dve(lambda e: e.tensor_copy(wts[:, :], bk[0:32, 0:128]), wait=[t, S.get(("wd", n - 1))], sig="v_wT")
            give(i, t)
            S["wd", n] = dma(w_dram[n % 2], wts[:, :], wait=[t, S.get(("wbl", n - 2))], sig=f"d_wd{n % 2}")

        def f_wb(n, ex):
            m = (8 * n + ex - 1) % NW
            S["wb", n, ex] = dma(
                wb_[m][:, :].rearrange("p (b q) -> p b q", b=4),
                w_dram[n % 2].rearrange("(b e) q -> e b q", b=4)[ex - 1].partition_broadcast(128),
                wait=[S["wd", n], S.get(("wbf", m))], sig=f"d_wb{m}")
            S["wbl", n] = S["wb", n, ex]

        def f_up(n, c):
            ex, cc = c // 4, c % 4
            k = CH * n + c
            bk = UPB[k % 2]
            h, l = fth_[n % 2], ftl_[n % 2]
            cols = slice(128 * cc, 128 * cc + 128)
            pe(lambda e: e.matmul(bk[:, :], uph[:, ex, cols], h[:, :], start=True, stop=False),
               wait=[S["ft", n], t_fw[ex], S.get(("gelu", k - 2))])
            pe(lambda e: e.matmul(bk[:, :], uph[:, ex, cols], l[:, :], start=False, stop=False))
            S["up", k] = pe(lambda e: e.matmul(bk[:, :], upl[:, ex, cols], h[:, :], start=False, stop=True), sig="m_up")
            if c == CH - 1:
                S["upd", n] = S["up", k]

        def f_gelu(n, c):
            ex, cc = c // 4, c % 4
            k = CH * n + c
            S["gelu", k] = act(lambda e: e.activation(gf_[k % 2][:, :], UPB[k % 2][:, :], ACT.Gelu,
                                                      bias=upb[:, ex, cc:cc + 1]),
                               wait=[S["up", k], t_ub, S.get(("lo", k - 2))], sig="a_ge")

        def f_hi(n, c):
            k = CH * n + c
            S["hi", k] = act(lambda e: e.activation(gh_[k % 3][:, :], gf_[k % 2][:, :], ACT.Copy),
                             wait=[S["gelu", k], S.get(("dn", k - 3))], sig="a_gh")

        def f_lo(n, c):
            k = CH * n + c
            S["lo", k] = dve(lambda e: e.tensor_tensor(gl_[k % 3][:, :], gf_[k % 2][:, :], f(gh_[k % 3][:, :]),
                                                       ALU.subtract),
                             wait=[S["hi", k], S.get(("dn", k - 3))], sig="v_gl")

        def f_down(n, c):
            ex, cc = c // 4, c % 4
            k = CH * n + c
            m = (EXPERTS * n + ex) % 2
            bk = DNB[m]
            h, l = gh_[k % 3], gl_[k % 3]
            pe(lambda e: e.matmul(bk[:, :], dnh[:, ex, cc, :], h[:, :], start=(cc == 0), stop=False),
               wait=[S["hi", k], S["lo", k], S.get(("eo", EXPERTS * n + ex - 2))])
            pe(lambda e: e.matmul(bk[:, :], dnl[:, ex, cc, :], h[:, :], start=False, stop=False))
            S["dn", k] = t = pe(lambda e: e.matmul(bk[:, :], dnh[:, ex, cc, :], l[:, :], start=False, stop=(cc == 3)),
                                sig="m_dn")
            if cc < 3:
                return
            q = EXPERTS * n + ex
            if ex == 0:
                S["eo", q] = dve(lambda e: e.tensor_scalar(acc[:, :], bk[:, :], dnb[:, 0:1], 0.1, ALU.add, ALU.mult),
                                 wait=[t, t_ub, S.get(("accT", n - 1))], sig="v_eo")
                S["acc"] = S["eo", q]
                return
            w = (8 * n + ex - 1) % NW
            S["eo", q] = dve(lambda e: e.scalar_tensor_tensor(
                out=eo_[q % 2][:, :], in0=bk[:, :], scalar=dnb[:, ex:ex + 1], in1=wb_[w][:, :],
                op0=ALU.add, op1=ALU.mult), wait=[t, S["wb", n, ex], S.get(("ea", q - 2))], sig="v_eo")
            S["wbf", w] = S["eo", q]
            S["ea", q] = pool(lambda e: e.tensor_tensor(acc[:, :], acc[:, :], eo_[q % 2][:, :], ALU.add),
                              wait=[S["eo", q], S["acc"]], sig="p_ac")
            S["acc"] = S["ea", q]

        def f_fin(n):
            i, bk, free = bank()
            for b in range(GB):
                t = pe(lambda e, b=b: e.transpose(bk[:, 128 * b:128 * b + 128], acc[:, 128 * b:128 * b + 128], ident),
                       wait=[S["acc"], free], sig="m_fT")
            S["accT", n] = t
            x1 = x1_[n % 2]
            t = dve(lambda e: e.tensor_reduce(am[:, :], bk[:, :].rearrange("p (b h) -> p b h", b=4), AX.X, ALU.max,
                                              apply_absolute_value=True), wait=[t], sig="v_fin")
            t = dve(lambda e: e.tensor_scalar(am[:, :], am[:, :], 1e-6, None, ALU.add), wait=[t], sig="v_fin")
            t = dve(lambda e: e.reciprocal(ar[:, :], am[:, :]), wait=[t], sig="v_fin")
            for b in range(GB):
                tt = dve(lambda e, b=b: e.scalar_tensor_tensor(
                    out=x1[:, b, :], in0=bk[:, 128 * b:128 * b + 128], scalar=ar[:, b:b + 1], in1=x1[:, b, :],
                    op0=ALU.mult, op1=ALU.add), wait=[t], sig="v_fin")
            give(i, tt)
            S["outd", n] = dma(out[GB * n:GB * n + GB].rearrange("b q d -> q b d"), x1[:, :, :], wait=[tt],
                               sig=f"d_out{n % 2}")

        plan = {}

        def at(slot, fn, *args):
            plan.setdefault(slot, []).append((fn, args))

        for n in range(NG):
            o = CH * n
            at(o + 0, a_ln, n)
            at(o + 0, a_ctx, n)
            at(o + 1, a_xhat, n)
            at(o + 2, a_xT, n)
            at(o + 3, a_xTs, n)
            if n + 1 < NG:
                at(o + 3, load_ctx, n + 1)
            for g in range(4):
                at(o + 2 + g, a_k, n, g)
                at(o + 4 + g, a_q, n, g)
            for b in range(GB):
                at(o + 8 + 3 * b - (b > 0), a_kblk, n, b)
                at(o + 8 + 3 * b, a_qblk, n, b) if b < 2 else at(o + 18 + 3 * (b - 2), a_qblk, n, b)
                at(o + 9 + 3 * b, a_A, n, b, 0)
                at(o + 9 + 3 * b, a_A, n, b, 1)
                at(o + 10 + 3 * b, a_A, n, b, 2)
                at(o + 10 + 3 * b, a_A, n, b, 3)
                at(o + 11 + 3 * b, a_nm, n, b)
                at(o + 12 + 3 * b, a_nmT, n, b)
                at(o + 13 + 3 * b, a_nmTe, n, b)
                at(o + 13 + 3 * b, a_V, n, b)
                for g in range(4):
                    at(o + 16 + 3 * b + g // 2, a_B, n, b, g)
                at(o + 18 + 3 * b, a_PV, n, b)
                at(o + 19 + 3 * b, a_norm, n, b)
                at(o + 20 + 3 * b, a_wo, n, b)
                at(o + 21 + 3 * b, a_x1, n, b)
            if n + 1 < NG:
                at(o + 31, load, n + 1)
            at(o + 31, a_ln2, n)
            at(o + 32, a_xn2, n)
            at(o + 33, a_x2T, n)
            at(o + 34, a_x2Ts, n)
            at(o + 35, a_router, n)
            at(o + 36, a_erT, n)
            at(o + 37, a_top1, n)
            at(o + 38, a_top2, n)
            at(o + 39, a_wT, n)
            for ex in range(1, EXPERTS):
                at(o + START + 4 * ex - 2, f_wb, n, ex)
            at(o + START + CH + 4, f_fin, n)

        for slot in range(START + CH * NG + 5):
            def ffn(fn, lag):
                k = slot - START - lag
                if 0 <= k < CH * NG:
                    fn(k // CH, k % CH)
            ffn(f_up, 0)
            ffn(f_hi, 1)
            for fn, args in plan.get(slot, []):
                fn(*args)
            ffn(f_gelu, 0)
            ffn(f_lo, 1)
            ffn(f_down, 2)

        block = ctx.enter_context(nc.Block())

        @block.sync
        def _(e):
            Q.play("sync", e)
            for p in range(2):
                e.wait_ge(Q.sems[f"d_out{p}"], Q.count[f"d_out{p}"])
                e.wait_ge(Q.sems[f"d_wd{p}"], Q.count[f"d_wd{p}"])

        @block.scalar
        def _(e):
            Q.play("scalar", e)

        @block.vector
        def _(e):
            Q.play("vector", e)

        @block.gpsimd
        def _(e):
            Q.play("gpsimd", e)

        @block.tensor
        def _(e):
            Q.play("tensor", e)


def kernel(**inputs):
    import concourse.bacc as bacc
    from concourse.bass_utils import run_bass_kernel_spmd

    def a(name):
        return np.asarray(inputs[name])

    def c(v):
        return np.ascontiguousarray(v)

    mask = c(a("mask_BxS2_bf0")).view(np.uint8)
    arrays = {
        "x": c(a("x")),
        "ctxT": c(a("ctx_1024").transpose(2, 0, 1).reshape(D, NB * LK)),
        "mask": mask.view(np.int32),
        "maskT": c(mask.T).view(np.int32),
        "wqT": c(a("L0_xattn_wq").T),
        "wkT": c(a("L0_xattn_wk").T),
        "wvT": c(a("L0_xattn_wv").T),
        "woT": c(a("L0_xattn_wo").T),
        "bqT": c(a("L0_xattn_bq").reshape(4, 4, 8).transpose(1, 2, 0).reshape(32, 4)),
        "bkT": c(a("L0_xattn_bk").reshape(4, 4, 8).transpose(1, 2, 0).reshape(32, 4)),
        "bv": c(a("L0_xattn_bv")),
        "bo": c(a("L0_xattn_bo")),
        "gate_w": c(a("L0_ffn_gate_w")),
        "gbias": c(a("L0_ffn_bias").reshape(8, 1)),
        "up_w": c(a("L0_ffn_up_w")),
        "up_bT": c(a("L0_ffn_up_b").reshape(8, 4, 128).transpose(2, 0, 1).reshape(128, 32)),
        "down_w": c(a("L0_ffn_down_w")),
        "down_bT": c(a("L0_ffn_down_b").T),
        "sw_up": c(a("L0_ffn_sw_up")),
        "sb_upT": c(a("L0_ffn_sb_up").reshape(4, 128).T),
        "sw_down": c(a("L0_ffn_sw_down")),
        "sb_downT": c(a("L0_ffn_sb_down").reshape(128, 1)),
        "consts": constants(),
    }
    nc = bacc.Bacc("TRN2", target_bir_lowering=False, num_devices=1)
    feeds, args = {}, []
    for name, v in arrays.items():
        feeds[f"in_{name}"] = v
        args.append(nc.dram_tensor(f"in_{name}", v.shape, mybir.dt.from_np(v.dtype), kind="ExternalInput").ap())
    args.append(nc.dram_tensor("out_0", (NB, LQ, D), F32, kind="ExternalOutput").ap())
    xattn_moe_kernel(nc, *args)
    r = run_bass_kernel_spmd(nc, [feeds], core_ids=[0])
    return r.results[0]["out_0"]
```

```python
from contextlib import ExitStack

import numpy as np

import concourse.bass as bass
from concourse import mybir

F32 = mybir.dt.float32
F32R = mybir.dt.float32r
BF16 = mybir.dt.bfloat16
U8 = mybir.dt.uint8
I32 = mybir.dt.int32
ALU = mybir.AluOpType
ACT = mybir.ActivationFunctionType
AX = mybir.AxisListType

NB, LQ, LK, D = 64, 128, 120, 128
NE, FF = 8, 512
GB = 4
NG = NB // GB
T = GB * LQ
TK = GB * LK
BIG = float(2.0 ** 100)
EPS = 1e-5
SCALE = float(1.0 / np.sqrt(8.0))
EXPERTS = NE + 1
CH = EXPERTS * 4

C_ID, C_CAUS, C_PRIO, C_ONES, C_TRIL, C_N = 0, 128, 248, 280, 408, 536
RG = 4
LAG = 3
GAP = 6
P0 = 12
START = P0 + 3 * GAP + 18
HI_ON_DVE = ()


def constants():
    c = np.zeros((128, C_N), np.float32)
    c[:, C_ID:C_ID + 128] = np.eye(128)
    q, k = np.arange(128)[:, None], np.arange(LK)[None, :]
    c[:, C_CAUS:C_CAUS + LK] = np.where(k > q, -BIG, 0.0)
    c[:, C_PRIO:C_PRIO + 32] = np.tile(8.0 - np.arange(8), 4)
    j = np.arange(4)[:, None]
    m = np.arange(32)[None, :]
    c[:, C_ONES:C_ONES + 128] = (m // 8 == j).astype(np.float32).reshape(-1)
    kk, qq = np.arange(128)[:, None], np.arange(128)[None, :]
    c[:, C_TRIL:C_TRIL + 128] = (kk <= qq)
    return c


class Queues:

    def __init__(self, sem):
        self.sem, self.sems, self.count = sem, {}, {}
        self.ops = {n: [] for n in ("tensor", "vector", "scalar", "gpsimd", "sync")}

    def add(self, engine, fn, wait=(), sig=None, by=1):
        token = None
        if sig is not None:
            if sig not in self.sems:
                self.sems[sig], self.count[sig] = self.sem(sig), 0
            self.count[sig] += by
            token = (sig, self.count[sig])
        self.ops[engine].append((fn, [w for w in wait if w is not None], sig, by))
        return token

    def play(self, engine, eng):
        seen = {}
        for fn, wait, sig, by in self.ops[engine]:
            for name, value in wait:
                if seen.get(name, 0) < value:
                    eng.wait_ge(self.sems[name], value)
                    seen[name] = value
            ins = fn(eng)
            if sig is not None:
                ins.then_inc(self.sems[sig], by)


def xattn_moe_kernel(nc, x, ctxT, mask, maskT, wqT, wkT, wvT, woT, bqT, bkT, bv, bo, gate_w, gbias,
                     up_w, up_bT, down_w, down_bT, sw_up, sb_upT, sw_down, sb_downT, consts, out):
    w_dram = nc.dram_tensor("w_scratch", (2, 32, 128), F32, kind="Internal").ap()
    q_dram = nc.dram_tensor("q_scratch", (2, 4, 32, T), F32, kind="Internal").ap()
    k_dram = nc.dram_tensor("k_scratch", (2, 4, 32, TK), F32, kind="Internal").ap()
    with ExitStack() as ctx:
        def sb(name, shape, dt=F32):
            return ctx.enter_context(nc.sbuf_tensor(name, shape, dt))

        Q = Queues(lambda n: ctx.enter_context(nc.semaphore(n)))

        def pe(fn, wait=(), sig=None):
            return Q.add("tensor", fn, wait, sig)

        def dve(fn, wait=(), sig=None):
            return Q.add("vector", fn, wait, sig)

        def act(fn, wait=(), sig=None):
            return Q.add("scalar", fn, wait, sig)

        def pool(fn, wait=(), sig=None):
            return Q.add("gpsimd", fn, wait, sig)

        def dma(dst, src, wait=(), sig=None, queue="sync"):
            return Q.add(queue, lambda e: e.dma_start(dst, src), wait, sig, 16)

        banks = [ctx.enter_context(nc.psum_tensor(f"bank{i}", [128, 512], F32)) for i in range(8)]
        UPB, DNB, ATT = banks[0:3], banks[3:4], banks[4:8]

        con = sb("con", [128, C_N])
        ident = con[:, C_ID:C_ID + 128]
        identb = sb("identb", [128, 128], BF16)
        trilb = sb("trilb", [128, 128], BF16)
        onesb = sb("onesb", [128, 128], BF16)
        vis = sb("vis", [128, 64], BF16)
        visi = sb("visi", [128, 16], I32)
        visu = visi[:, :].bitcast(U8)
        poison = sb("poison", [128, 64])
        pz = sb("pz", [128, 64])
        pt_ = sb("pt_", [128, 2])
        nhalf = sb("nhalf", [128, 4])

        uph = sb("uph", [128, EXPERTS, FF], F32R)
        upl = sb("upl", [128, EXPERTS, FF], F32R)
        dnh = sb("dnh", [128, EXPERTS, 4, 128], F32R)
        dnl = sb("dnl", [128, EXPERTS, 4, 128], F32R)
        upb = sb("upb", [128, EXPERTS, 4])
        dnb = sb("dnb", [128, EXPERTS])
        wqh = sb("wqh", [128, 128], F32R)
        wql = sb("wql", [128, 128], F32R)
        wkh = sb("wkh", [128, 128], F32R)
        wkl = sb("wkl", [128, 128], F32R)
        wv = sb("wv", [128, 128])
        wo = sb("wo", [128, 128])
        bqk = sb("bqk", [128, 2])
        bvb = sb("bvb", [128, 128])
        bob = sb("bob", [128, 128])
        gwf = sb("gwf", [128, 8])
        gwh = sb("gwh", [128, 8], F32R)
        gwl = sb("gwl", [128, 8], F32R)
        gb = sb("gb", [8, 1])
        ngb = sb("ngb", [8, 1])

        xs_ = [sb(f"x{i}", [128, GB, 128]) for i in range(2)]
        x1_ = [sb(f"x1_{i}", [128, GB, 128]) for i in range(2)]
        xhat = sb("xhat", [128, GB, 128])
        xth = sb("xth", [128, T], F32R)
        xtl = sb("xtl", [128, T], F32R)
        fth_ = [sb(f"fth{i}", [128, T], F32R) for i in range(2)]
        ftl_ = [sb(f"ftl{i}", [128, T], F32R) for i in range(2)]
        cxf = sb("cxf", [128, TK])
        cxh, cxl = xth[:, 0:TK], xtl[:, 0:TK]
        st = sb("st", [128, GB, 6])
        mv = sb("mv", [128, GB, 2])
        ve = sb("ve", [128, GB])
        rstd = sb("rstd", [128, GB])
        st2 = sb("st2", [128, GB, 6])
        mv2 = sb("mv2", [128, GB, 2])
        ve2 = sb("ve2", [128, GB])
        rstd2 = sb("rstd2", [128, GB])
        keyb = [sb(f"keyb{i}", [128, GB, LK // 4], I32) for i in range(2)]
        maskb = sb("maskb", [128, GB, LK], BF16)
        px = sb("px", [128, T])
        ph = sb("ph", [128, T], F32R)
        pl = sb("pl", [128, T], F32R)
        vv = sb("vv", [128, GB, 128])
        qst = sb("qst", [128, 4, T], F32R)
        kst = sb("kst", [128, 4, TK], F32R)
        kblk = sb("kblk", [128, 4, 4, LK], F32R)
        qblk_ = [sb(f"qblk{i}", [128, 4, 4, 128], F32R) for i in range(2)]
        NP = 5
        prob = [sb(f"prob{i}", [128, 512]) for i in range(NP)]
        vm_ = [sb(f"vm{i}", [128, 16, 32]) for i in range(2)]
        nm = sb("nm", [128, 16])
        nmh = sb("nmh", [128, 16], F32R)
        nm2 = sb("nm2", [128, 16, 2])
        nmt = sb("nmt", [8, 4, 128], F32R)
        rsum = sb("rsum", [128, 128])
        oT = sb("oT", [128, 128])
        er = sb("er", [8, T])
        s1 = sb("s1", [128, 4, 8])
        s2 = sb("s2", [128, 4, 8])
        eq = sb("eq", [128, 4, 8])
        oh1 = sb("oh1", [128, 4, 8])
        oh2 = sb("oh2", [128, 4, 8])
        m1 = sb("m1", [128, 4])
        m2 = sb("m2", [128, 4])
        pm = sb("pm", [128, 4])
        wgt = sb("wgt", [128, 4, 8])
        wts = sb("wts", [32, 128])
        NW = 2
        wb_ = [sb(f"wb{i}", [128, T]) for i in range(NW)]
        gf_ = [sb(f"gf{i}", [128, T]) for i in range(2)]
        gh_ = [sb(f"gh{i}", [128, T], F32R) for i in range(RG)]
        gl_ = [sb(f"gl{i}", [128, T], F32R) for i in range(RG)]
        eo_ = [sb(f"eo{i}", [128, T]) for i in range(2)]
        acc = sb("acc", [128, T])
        am = sb("am", [128, 4])
        ar = sb("ar", [128, 4])

        def f(ap):
            return ap.bitcast(F32)

        spare = [(i, None) for i in range(len(ATT))]

        def bank():
            i, last_read = spare.pop(0)
            return i, ATT[i], last_read

        def give(i, last_read):
            spare.append((i, last_read))

        t_con = dma(con[:, :], consts, sig="d_con")
        for dst, src in ((wv[:, :], wvT), (wo[:, :], woT), (gwf[:, :], gate_w), (gb[:, :], gbias),
                         (bvb[:, :], bv.partition_broadcast(128)), (bob[:, :], bo.partition_broadcast(128)),
                         (xhat[:, 0, :], wqT), (xhat[:, 1, :], wkT)):
            t_small = dma(dst, src, sig="d_small")
        t_bias = dma(bqk[:, 0:1], bqT, sig="d_bias")
        t_bias = dma(bqk[:, 1:2], bkT, sig="d_bias")

        t_load = {}

        def load(n):
            p = n % 2
            prev = t_free_x.get(n - 2)
            dma(xs_[p][:, :, :], x[GB * n:GB * n + GB].rearrange("b q d -> q b d"), wait=[prev], sig=f"d_x{p}")
            t_load[n] = dma(keyb[p][:, :, :], mask[GB * n:GB * n + GB, :].partition_broadcast(128),
                            wait=[t_mask.get(n - 2)], sig=f"d_x{p}")

        def load_ctx(n):
            t_ctx[n] = dma(cxf[:, :], ctxT[:, TK * n:TK * n + TK], wait=[t_cxl.get(n - 1), S.get(("cx", n - 1))], sig="d_ctx")

        S = {}
        t_free_x, t_mask, t_ctx, t_cxl = {}, {}, {}, {}
        load(0)
        load_ctx(0)
        t_vis = dma(visi[0:LK, :], maskT, sig="d_vis")
        t_ub = dma(upb[:, 0, :], sb_upT, sig="d_fb")
        t_ub = dma(upb[:, 1:, :], up_bT.rearrange("p (e c) -> p e c", e=8), sig="d_fb")
        t_ub = dma(dnb[:, 0:1], sb_downT, sig="d_fb")
        t_ub = dma(dnb[:, 1:], down_bT, sig="d_fb")

        t_nh = pool(lambda e: e.memset(nhalf[:, :], -0.5), sig="p_nh")
        t_z = pool(lambda e: e.memset(f(kblk[:, :, :, :]), 0.0), sig="p_zk")
        t_zq = None
        for qb in qblk_:
            t_zq = pool(lambda e, qb=qb: e.memset(f(qb[:, :, :, :]), 0.0), sig="p_zq")
        t_zs = pool(lambda e: e.memset(f(qst[:, :, :]), 0.0), sig="p_zs")
        t_zs2 = pool(lambda e: e.memset(f(kst[:, :, :]), 0.0), sig="p_zs")
        t_o = pool(lambda e: e.memset(f(ph[0:2, 0:TK]), 1.0), sig="p_zs")
        for j in range(4):
            t_tail = dma(f(kst[32 * j + 24:32 * j + 26, :, :]),
                         f(ph[0:2, 0:TK]).unsqueeze(1).to_broadcast([2, 4, TK]), wait=[t_zs2, t_o], sig="d_tail")
        S["pd"] = t_tail
        for v in vm_:
            t_zv = pool(lambda e, v=v: e.memset(v[:, :, :], 0.0), sig="p_zv")
        t_one = pool(lambda e: e.memset(onesb[:, :], 1.0), sig="p_one")

        for src, wh, wl in ((0, wqh, wql), (1, wkh, wkl)):
            t = dve(lambda e, wh=wh, src=src: e.tensor_copy(wh[:, :], xhat[:, src, :]), wait=[t_small], sig="v_wh")
            t_w = dve(lambda e, wh=wh, wl=wl, src=src: e.tensor_tensor(wl[:, :], xhat[:, src, :], f(wh[:, :]),
                                                                       ALU.subtract), wait=[t], sig="v_wl")
        t = dve(lambda e: e.tensor_copy(gwh[:, :], gwf[:, :]), sig="v_gw")
        dve(lambda e: e.tensor_tensor(gwl[:, :], gwf[:, :], f(gwh[:, :]), ALU.subtract), wait=[t], sig="v_gw")
        t_gw = dve(lambda e: e.tensor_scalar(ngb[:, :], gb[:, :], -1.0, None, ALU.mult), sig="v_gw")
        dve(lambda e: e.tensor_copy(identb[:, :], ident), wait=[t_con], sig="v_id")
        t_id = dve(lambda e: e.tensor_copy(trilb[:, :], con[:, C_TRIL:C_TRIL + 128]), sig="v_id")

        t = dve(lambda e: e.tensor_scalar(vis[0:LK, :], visu[0:LK, :], -1.0, 1.0, ALU.mult, ALU.add),
                wait=[t_vis], sig="v_vis")
        i, bk, free = bank()
        pe(lambda e, bk=bk: e.matmul(bk[:, 0:64], trilb[0:LK, :], vis[0:LK, :], start=True, stop=True),
           wait=[t, t_id, t_one])
        t = pe(lambda e, bk=bk: e.matmul(bk[:, 64:128], onesb[0:LK, :], vis[0:LK, :], start=True, stop=True,
                                         skip_group_check=True), sig="m_vis")
        dve(lambda e, bk=bk: e.tensor_reduce(pt_[:, 0:1], bk[:, 64:128], AX.X, ALU.add), wait=[t], sig="v_poi")
        t = dve(lambda e, bk=bk: e.tensor_scalar(pz[:, :], bk[:, 0:64], 0.0, 3e38, ALU.is_equal, ALU.mult), sig="v_poi")
        give(i, t)
        t = dve(lambda e: e.tensor_scalar(pt_[:, 1:2], pt_[:, 0:1], 0.0, None, ALU.is_gt), wait=[t], sig="v_poi")
        t = dve(lambda e: e.tensor_scalar(poison[:, :], pz[:, :], pt_[:, 1:2], 10.0, ALU.mult, ALU.mult),
                wait=[t], sig="v_poi")
        t_poison = dve(lambda e: e.tensor_tensor(pz[:, :], poison[:, :], poison[:, :], ALU.subtract),
                       wait=[t], sig="v_poi")

        stage_free = [None] * NP
        t_fw = {}
        k = 0
        for ex in range(EXPERTS):
            for what in range(2):
                s = prob[k % NP]
                if what == 0:
                    src = sw_up if ex == 0 else up_w[ex - 1]
                    dst = s[:, :]
                    h, l = uph[:, ex, :], upl[:, ex, :]
                else:
                    src = (sw_down if ex == 0 else down_w[ex - 1]).rearrange("(c p) h -> p c h", p=128)
                    dst = s[:, :].rearrange("p (c h) -> p c h", c=4)
                    h = dnh[:, ex, :, :].rearrange("p c h -> p (c h)")
                    l = dnl[:, ex, :, :].rearrange("p c h -> p (c h)")
                td = dma(dst, src, wait=[stage_free[k % NP]], sig=f"d_w{k % NP}")
                ta = act(lambda e, h=h, s=s: e.activation(h, s[:, :], ACT.Copy), wait=[td], sig="a_wh")
                tp = pool(lambda e, h=h, l=l, s=s: e.tensor_tensor(l, s[:, :], f(h), ALU.subtract),
                          wait=[ta, td], sig="p_wl")
                stage_free[k % NP] = tp
                t_fw[ex] = tp
                k += 1
        for i in range(NP):
            t_zp = pool(lambda e, i=i: e.memset(prob[i][:, :], 0.0), wait=[stage_free[i]], sig="p_zp")

        def ln_a(n, src, stats, agg, v, wait, tag):
            for b in range(GB):
                t = dve(lambda e, b=b: e.bn_stats(stats[:, b, :], src[:, b, :]), wait=wait, sig=f"v_st{tag}")
            for b in range(GB):
                t = dve(lambda e, b=b: e.bn_aggr(agg[:, b, :], stats[:, b, :]), wait=[t], sig=f"v_ag{tag}")
            return dve(lambda e: e.tensor_scalar(v[:, :], agg[:, :, 1], EPS, None, ALU.add),
                       wait=[t], sig=f"v_ve{tag}")

        def a_ln(n):
            xt = xs_[n % 2]
            t = ln_a(n, xt, st, mv, ve, [t_load[n], t_w], "1")
            S["rs", n] = pool(lambda e: e.tensor_tensor(rstd[:, :], ve[:, :], nhalf[:, :], ALU.pow),
                              wait=[t, t_nh, S.get(("xhat", n - 1))], sig="p_rs1")

        def a_msk(n):
            S["msk", n] = dve(lambda e: e.scalar_tensor_tensor(
                out=maskb[:, :, :], in0=keyb[n % 2][:, :, :].bitcast(U8), scalar=-BIG,
                in1=con[:, C_CAUS:C_CAUS + LK].unsqueeze(1).to_broadcast([128, GB, LK]),
                op0=ALU.mult, op1=ALU.min), wait=[t_con, t_load[n], S.get(("Bd", n - 1, 3))], sig="v_msk")
            t_mask[n] = S["msk", n]

        def a_ctx(n):
            t = act(lambda e: e.activation(cxh, cxf[:, :], ACT.Copy), wait=[t_ctx[n], S.get(("Qp", n - 1))],
                    sig="a_ch")
            S["cx", n] = dve(lambda e: e.tensor_tensor(cxl, cxf[:, :], f(cxh), ALU.subtract), wait=[t], sig="v_cl")

        def a_xhat(n):
            xt = xs_[n % 2]
            for b in range(GB):
                t = dve(lambda e, b=b: e.tensor_scalar(
                    xhat[:, b, :], xt[:, b, :], mv[:, b, 0:1], rstd[:, b:b + 1], ALU.subtract, ALU.mult),
                    wait=[S["rs", n], S.get(("xt2", n - 1))], sig="v_xh")
            S["xhat", n] = t
            S["xb", n] = pool(lambda e: e.tensor_tensor(
                xt[:, :, :], xt[:, :, :], bob[:, :].unsqueeze(1).to_broadcast([128, GB, 128]), ALU.add),
                wait=[t, t_small], sig="p_xb")

        def tr4(src, wait, sig):
            i, bk, free = bank()
            for b in range(GB):
                t = pe(lambda e, b=b: e.transpose(bk[:, 128 * b:128 * b + 128], src[:, b, :], ident),
                       wait=[*wait, free], sig=sig)
            return i, bk, t

        def split(n, i, bk, t, hi, lo, wait, tag):
            th = act(lambda e: e.activation(hi[:, :], bk[:, :], ACT.Copy), wait=[t, *wait], sig=f"a_{tag}")
            tl = dve(lambda e: e.tensor_tensor(lo[:, :], bk[:, :], f(hi[:, :]), ALU.subtract),
                     wait=[th, *wait], sig=f"v_{tag}")
            give(i, tl)
            return tl

        def a_xT(n):
            S["xT", n] = i, bk, t = tr4(xhat, [S["xhat", n], t_con], "m_xT")
            S["xt1", n] = t

        def a_xTs(n):
            i, bk, t = S["xT", n]
            S["xt", n] = split(n, i, bk, t, xth, xtl, [S["Kp", n]], "xt")

        def project(n, wh, wl, ch, cl, N, wait, col, dram, dst, free_dst, tag):
            i, bk, free = bank()
            pe(lambda e: e.matmul(bk[:, 0:N], wh[:, :], ch, start=True, stop=False), wait=[*wait, t_w, free])
            pe(lambda e: e.matmul(bk[:, 0:N], wh[:, :], cl, start=False, stop=False))
            S[tag + "p", n] = t = pe(lambda e: e.matmul(bk[:, 0:N], wl[:, :], ch, start=False, stop=True),
                                     sig=f"m_{tag}")
            ta = act(lambda e: e.activation(px[:, 0:N], bk[:, 0:N], ACT.Identity, bias=bqk[:, col:col + 1]),
                     wait=[t, t_bias, S.get("px")], sig=f"a_{tag}")
            give(i, ta)
            th = dve(lambda e: e.tensor_copy(ph[:, 0:N], px[:, 0:N]), wait=[ta, S.get("pd")], sig=f"v_{tag}h")
            S["px"] = tl = dve(lambda e: e.tensor_tensor(pl[:, 0:N], px[:, 0:N], f(ph[:, 0:N]), ALU.subtract),
                               wait=[th, S.get("pd")], sig=f"v_{tag}l")
            dma(dram[0].rearrange("g r t -> (g r) t"), f(ph[:, 0:N]), wait=[th, S.get(("stk" + tag, n - 1))], sig=f"d_{tag}w")
            td = dma(dram[1].rearrange("g r t -> (g r) t"), f(pl[:, 0:N]), wait=[tl], sig=f"d_{tag}w")
            S["pd"] = td
            S["w" + tag, n] = td

        def stack(n, dram, parts, dst, free_dst, tag):
            for j in range(4):
                for part, hl in enumerate(parts):
                    r = 32 * j + 8 * part
                    t = dma(f(dst[r:r + 8, :, :]), dram[hl, :, 8 * j:8 * j + 8, :].rearrange("g d t -> d g t"),
                            wait=[S["w" + tag, n], free_dst, t_tail], sig=f"d_{tag}s")
            S["stk" + tag, n] = t

        def a_k(n):
            project(n, wkh, wkl, cxh, cxl, TK, [S["cx", n]], 1, k_dram, kst, None, "K")

        def a_ks(n):
            stack(n, k_dram, (0, 1, 0), kst, S.get(("Bd", n - 1, 3)), "K")

        def a_q(n):
            project(n, wqh, wql, xth[:, :], xtl[:, :], T, [S["xt", n]], 0, q_dram, qst, None, "Q")

        def a_qs(n):
            stack(n, q_dram, (0, 0, 1), qst, S.get(("qst_free", n - 1)), "Q")

        def a_kblk(n, b):
            t = None
            for j in range(4):
                t = dma(f(kblk[32 * j:32 * j + 32, :, j, :]), f(kst[32 * j:32 * j + 32, :, LK * b:LK * b + LK]),
                        wait=[S["stkK", n], S.get(("Ad", prev(n, b))), t_z, t_tail], sig="d_kb")
            S["kb", n, b] = t
            S["kbl", n] = t

        def prev(n, b, back=1):
            return GB * n + b - back

        def a_qblk(n, b):
            q = (GB * n + b) % 2
            for j in range(4):
                t = dma(f(qblk_[q][32 * j:32 * j + 24, :, j, :]), f(qst[32 * j:32 * j + 24, :, 128 * b:128 * b + 128]),
                        wait=[S["stkQ", n], S.get(("Bdone", prev(n, b, 2))), t_zq], sig=f"d_qb{q}")
            S["qcopied"] = t

        def a_A(n, b, g):
            i, bk, free = bank()
            pe(lambda e: e.matmul(bk[:, 0:480], qst[:, g, 128 * b:128 * b + 128],
                                  kblk[:, g, :, :].rearrange("p a b -> p (a b)"), start=True, stop=False),
               wait=[S["kb", n, b], S["stkQ", n], t_zs, free])
            t = pe(lambda e: e.matmul(bk[:, 0:480].rearrange("p (j k) -> p j k", j=4), identb[:, :],
                                      maskb[:, b, :].unsqueeze(1).to_broadcast([128, 4, LK]), start=False, stop=True),
                   wait=[S["msk", n], t_id], sig="m_A")
            tm = dve(lambda e: e.tensor_reduce(nm[:, 4 * g:4 * g + 4], bk[:, 0:480].rearrange("p (j k) -> p j k", j=4),
                                               AX.X, ALU.max, negate=True),
                     wait=[t, S.get("nm_free")], sig="v_mx")
            give(i, tm)
            S["mx", n, b] = tm
            S["Ad", GB * n + b] = t
            if b == 3:
                S["Aend", n] = t

        def a_nm(n, b):
            t = dve(lambda e: e.tensor_copy(nmh[:, :], nm[:, :]), wait=[S["mx", n, b]], sig="v_nm")
            dve(lambda e: e.tensor_copy(nm2[:, :, 0], f(nmh[:, :])), wait=[t, S.get("nmT_read")], sig="v_nm")
            S["nm", n, b] = dve(lambda e: e.tensor_tensor(nm2[:, :, 1], nm[:, :], f(nmh[:, :]), ALU.subtract),
                                wait=[t, S.get("nmT_read")], sig="v_nm")
            S["nm_free"] = S["nm", n, b]

        def a_nmT(n, b):
            i, bk, free = bank()
            for g in range(4):
                t = pe(lambda e, g=g: e.transpose(bk[0:8, 128 * g:128 * g + 128],
                                                  nm2[:, 4 * g:4 * g + 4, :].rearrange("p a b -> p (a b)"), ident),
                       wait=[S["nm", n, b], free], sig="m_nT")
            S["nmT_read"] = t
            S["nmT", n, b] = i, bk, t

        def a_nmTe(n, b):
            i, bk, t = S["nmT", n, b]
            te = dve(lambda e: e.tensor_copy(nmt[:, :, :], bk[0:8, :].rearrange("p (g q) -> p g q", g=4)),
                     wait=[t, S.get("nmt_free")], sig="v_nT")
            give(i, te)
            q = (GB * n + b) % 2
            for j in range(4):
                t = dma(f(qblk_[q][32 * j + 24:32 * j + 26, :, j, :]), f(nmt[2 * j:2 * j + 2, :, :]),
                        wait=[te, S.get(("Bdone", prev(n, b, 2))), t_zq], sig=f"d_qb{q}")
            S["qb", n, b] = t
            S["nmt_free"] = t

        def a_V(n):
            i, bk, free = bank()
            for b in range(GB):
                t = pe(lambda e, b=b: e.matmul(bk[0:LK, 128 * b:128 * b + 128], cxf[:, LK * b:LK * b + LK], wv[:, :],
                                               start=True, stop=True, skip_group_check=True),
                       wait=[t_ctx[n], t_small, free], sig="m_V")
            S["Vp", n] = t
            t_cxl[n] = t
            te = dve(lambda e: e.tensor_tensor(
                vv[0:LK, :, :], bk[0:LK, :].rearrange("p (b d) -> p b d", b=4),
                bvb[0:LK, :].unsqueeze(1).to_broadcast([LK, GB, 128]), ALU.add),
                wait=[t, t_small, S.get(("vm", n - 1, 3))], sig="v_V")
            give(i, te)
            S["V", n] = te

        def a_vm(n, b):
            vm = vm_[(GB * n + b) % 2]
            for j in range(4):
                t = pool(lambda e, j=j: e.tensor_copy(
                    vm[0:LK, :, :].rearrange("p (g j) m -> p g j m", g=4)[:, :, j, 8 * j:8 * j + 8],
                    vv[0:LK, b, :].rearrange("p (g j d) -> p g j d", g=4, j=4)[:, :, j, :]),
                    wait=[S["V", n], t_zv, S.get(("PVd", prev(n, b, 2)))], sig="p_vm")
            S["vm", n, b] = t

        def a_B(n, b, g):
            i, bk, free = bank()
            q = (GB * n + b) % 2
            s = (4 * (GB * n + b) + g) % NP
            pe(lambda e: e.matmul(bk[0:LK, :], kst[:, g, LK * b:LK * b + LK],
                                  qblk_[q][:, g, :, :].rearrange("p a b -> p (a b)"), start=True, stop=False),
               wait=[S["qb", n, b], free])
            t = pe(lambda e: e.matmul(bk[0:LK, :].rearrange("p (j k) -> p j k", j=4), maskb[:, b, :],
                                      identb[:, :].unsqueeze(1).to_broadcast([128, 4, 128]), start=False, stop=True),
                   sig="m_B")
            S["Bdone", GB * n + b] = t
            S["Bd", n, b] = t
            te = act(lambda e: e.activation(prob[s][0:LK, :], bk[0:LK, :], ACT.Exp, scale=SCALE),
                     wait=[t, S.get(("pfree", s)), t_zp], sig="a_ex")
            give(i, te)
            S["P", n, b, g] = te

        ones32 = con[:, C_ONES:C_ONES + 128].rearrange("p (j m) -> p j m", j=4)

        def a_PV(n, b):
            i, bk, free = bank()
            vm = vm_[(GB * n + b) % 2]
            for half in range(2):
                for j in range(4):
                    for g in range(4):
                        s = (4 * (GB * n + b) + g) % NP
                        w = vm[:, 4 * g + j, :] if half == 0 else ones32[:, j, :]
                        t = pe(lambda e, g=g, j=j, s=s, w=w, half=half: e.matmul(
                            bk[32 * g:32 * g + 32, 128 * half:128 * half + 128], w,
                            prob[s][:, 128 * j:128 * j + 128], start=(j == 0), stop=(j == 3), skip_group_check=True),
                            wait=[S["P", n, b, g], S["vm", n, b], free, t_zp],
                            sig="m_PV")
                        if half == 1 and j == 3:
                            S["pfree", s] = t
            S["PVd", GB * n + b] = t
            S["PV", n, b] = i, bk, t

        def a_norm(n, b):
            i, bk, t = S["PV", n, b]
            tr = dve(lambda e: e.reciprocal(rsum[:, :], bk[:, 128:256]), wait=[t, S.get("oT")], sig="v_rs")
            to = dve(lambda e: e.tensor_tensor(oT[:, :], bk[:, 0:128], rsum[:, :], ALU.mult),
                     wait=[tr, S.get("Wo")], sig="v_oT")
            give(i, to)
            S["oT"] = to

        def a_wo(n, b):
            i, bk, free = bank()
            t = pe(lambda e: e.matmul(bk[:, 0:128], oT[:, :], wo[:, :], start=True, stop=True),
                   wait=[S["oT"], t_small, free], sig="m_wo")
            S["Wo"] = t
            S["wo", n, b] = i, bk, t

        def a_x1(n, b):
            i, bk, t = S["wo", n, b]
            xt, x1 = xs_[n % 2], x1_[n % 2]
            t = dve(lambda e: e.scalar_tensor_tensor(
                out=x1[:, b, :], in0=bk[:, 0:128], scalar=pz[:, GB * n + b:GB * n + b + 1], in1=xt[:, b, :],
                op0=ALU.add, op1=ALU.add), wait=[t, S["xb", n], t_poison, S.get(("outd", n - 2))], sig="v_x1")
            give(i, t)
            S["x1", n] = t
            if b == 3:
                t_free_x[n] = t

        def a_ln2(n):
            t = ln_a(n, x1_[n % 2], st2, mv2, ve2, [S["x1", n]], "2")
            S["rs2", n] = pool(lambda e: e.tensor_tensor(rstd2[:, :], ve2[:, :], nhalf[:, :], ALU.pow),
                               wait=[t, S.get(("xh2", n - 1))], sig="p_rs2")

        def a_xn2(n):
            x1 = x1_[n % 2]
            for b in range(GB):
                t = dve(lambda e, b=b: e.tensor_scalar(
                    xhat[:, b, :], x1[:, b, :], mv2[:, b, 0:1], rstd2[:, b:b + 1], ALU.subtract, ALU.mult),
                    wait=[S["rs2", n], S["xt1", n]], sig="v_xh2")
            S["xh2", n] = t

        def a_x2T(n):
            S["x2T", n] = i, bk, t = tr4(xhat, [S["xh2", n]], "m_x2T")
            S["xt2", n] = t

        def a_x2Ts(n):
            i, bk, t = S["x2T", n]
            S["ft", n] = split(n, i, bk, t, fth_[n % 2], ftl_[n % 2],
                               [S.get(("upd", n - 2)), S.get(("rt", n - 2))], "ft")

        def a_router(n):
            i, bk, free = bank()
            h, l = fth_[n % 2], ftl_[n % 2]
            pe(lambda e: e.matmul(bk[0:8, :], gwh[:, :], h[:, :], start=True, stop=False),
               wait=[S["ft", n], t_gw, free])
            pe(lambda e: e.matmul(bk[0:8, :], gwl[:, :], h[:, :], start=False, stop=False))
            t = pe(lambda e: e.matmul(bk[0:8, :], gwh[:, :], l[:, :], start=False, stop=True), sig="m_rt")
            S["rt", n] = t
            S["er", n] = act(lambda e: e.activation(er[:, :], bk[0:8, :], ACT.Exp, scale=-1.0, bias=ngb[:, 0:1]),
                             wait=[t, t_gw, S.get(("erT", n - 1))], sig="a_er")
            give(i, S["er", n])

        def a_erT(n):
            i, bk, free = bank()
            for b in range(GB):
                t = pe(lambda e, b=b: e.transpose(bk[:, 8 * b:8 * b + 8], er[:, 128 * b:128 * b + 128], ident[0:8, 0:8]),
                       wait=[S["er", n], free], sig="m_eT")
            S["erT", n] = t
            t = dve(lambda e: e.tensor_scalar(s2[:, :, :], bk[:, 0:32].rearrange("p (b e) -> p b e", b=4), 1.0, None,
                                              ALU.add), wait=[t], sig="v_top")
            give(i, t)
            S["top"] = dve(lambda e: e.reciprocal(s1[:, :, :], s2[:, :, :]), wait=[t], sig="v_top")

        prio = con[:, C_PRIO:C_PRIO + 32].rearrange("p (b e) -> p b e", b=4)

        def bc(a):
            return a[:, :].unsqueeze(2).to_broadcast([128, 4, 8])

        def first(src, m, oh):
            def step(fn):
                S["top"] = dve(fn, wait=[S["top"]], sig="v_top")
            step(lambda e: e.tensor_reduce(m[:, :], src[:, :, :], AX.X, ALU.max))
            step(lambda e: e.tensor_tensor(eq[:, :, :], src[:, :, :], bc(m), ALU.is_equal))
            step(lambda e: e.tensor_tensor(eq[:, :, :], eq[:, :, :], prio, ALU.mult))
            step(lambda e: e.tensor_reduce(pm[:, :], eq[:, :, :], AX.X, ALU.max))
            step(lambda e: e.tensor_tensor(oh[:, :, :], eq[:, :, :], bc(pm), ALU.is_equal))

        def a_top1(n):
            first(s1, m1, oh1)
            S["top"] = dve(lambda e: e.scalar_tensor_tensor(
                out=s2[:, :, :], in0=oh1[:, :, :], scalar=-4.0, in1=s1[:, :, :], op0=ALU.mult, op1=ALU.add),
                wait=[S["top"]], sig="v_top")

        def a_top2(n):
            first(s2, m2, oh2)

            def step(fn, wait=()):
                S["top"] = dve(fn, wait=[S["top"], *wait], sig="v_top")
            step(lambda e: e.tensor_tensor(oh1[:, :, :], oh1[:, :, :], oh2[:, :, :], ALU.add))
            step(lambda e: e.tensor_tensor(s1[:, :, :], s1[:, :, :], oh1[:, :, :], ALU.mult))
            step(lambda e: e.scalar_tensor_tensor(out=m1[:, :], in0=m1[:, :], scalar=1e-6, in1=m2[:, :],
                                                  op0=ALU.add, op1=ALU.add))
            step(lambda e: e.reciprocal(m2[:, :], m1[:, :]))
            step(lambda e: e.scalar_tensor_tensor(out=wgt[:, :, :], in0=s1[:, :, :], scalar=0.1, in1=bc(m2),
                                                  op0=ALU.mult, op1=ALU.mult), wait=[S.get("wT")])

        def a_wT(n):
            i, bk, free = bank()
            S["wT"] = t = pe(lambda e: e.transpose(bk[0:32, 0:128], wgt[:, :, :].rearrange("p b e -> p (b e)"), ident),
                             wait=[S["top"], free], sig="m_wT")
            t = dve(lambda e: e.tensor_copy(wts[:, :], bk[0:32, 0:128]), wait=[t, S.get(("wd", n - 1))], sig="v_wT")
            give(i, t)
            S["wd", n] = dma(w_dram[n % 2], wts[:, :], wait=[t, S.get(("wbl", n - 2))], sig=f"d_wd{n % 2}")

        def f_wb(n, ex):
            m = (8 * n + ex - 1) % NW
            S["wb", n, ex] = dma(
                wb_[m][:, :].rearrange("p (b q) -> p b q", b=4),
                w_dram[n % 2].rearrange("(b e) q -> e b q", b=4)[ex - 1].partition_broadcast(128),
                wait=[S["wd", n], S.get(("wbf", m))], sig=f"d_wb{m}")
            S["wbl", n] = S["wb", n, ex]

        def f_up(n, c):
            ex, cc = c // 4, c % 4
            k = CH * n + c
            bk = UPB[k % 3]
            h, l = fth_[n % 2], ftl_[n % 2]
            cols = slice(128 * cc, 128 * cc + 128)
            pe(lambda e: e.matmul(bk[:, :], uph[:, ex, cols], h[:, :], start=True, stop=False),
               wait=[S["ft", n], t_fw[ex], S.get(("gelu", k - 3))])
            pe(lambda e: e.matmul(bk[:, :], uph[:, ex, cols], l[:, :], start=False, stop=False))
            S["up", k] = pe(lambda e: e.matmul(bk[:, :], upl[:, ex, cols], h[:, :], start=False, stop=True), sig="m_up")
            if c == CH - 1:
                S["upd", n] = S["up", k]

        def f_gelu(n, c):
            ex, cc = c // 4, c % 4
            k = CH * n + c
            S["gelu", k] = act(lambda e: e.activation(gf_[k % 2][:, :], UPB[k % 3][:, :], ACT.Gelu,
                                                      bias=upb[:, ex, cc:cc + 1]),
                               wait=[S["up", k], t_ub, S.get(("lo", k - 2))], sig="a_ge")

        def f_hi(n, c):
            k = CH * n + c
            wait = [S["gelu", k], S.get(("dn", k - RG))]
            if k % 6 in HI_ON_DVE:
                S["hi", k] = dve(lambda e: e.tensor_copy(gh_[k % RG][:, :], gf_[k % 2][:, :]), wait=wait, sig="v_gh")
            else:
                S["hi", k] = act(lambda e: e.activation(gh_[k % RG][:, :], gf_[k % 2][:, :], ACT.Copy), wait=wait,
                                 sig="a_gh")

        def f_lo(n, c):
            k = CH * n + c
            S["lo", k] = dve(lambda e: e.tensor_tensor(gl_[k % RG][:, :], gf_[k % 2][:, :], f(gh_[k % RG][:, :]),
                                                       ALU.subtract),
                             wait=[S["hi", k], S.get(("dn", k - RG))], sig="v_gl")

        def f_down(n, c):
            ex, cc = c // 4, c % 4
            k = CH * n + c
            bk = DNB[0]
            h, l = gh_[k % RG], gl_[k % RG]
            pe(lambda e: e.matmul(bk[:, :], dnh[:, ex, cc, :], h[:, :], start=(cc == 0), stop=False),
               wait=[S["hi", k], S["lo", k], S.get(("eo", EXPERTS * n + ex - 1))])
            pe(lambda e: e.matmul(bk[:, :], dnl[:, ex, cc, :], h[:, :], start=False, stop=False))
            S["dn", k] = t = pe(lambda e: e.matmul(bk[:, :], dnh[:, ex, cc, :], l[:, :], start=False, stop=(cc == 3)),
                                sig="m_dn")
            if cc < 3:
                return
            q = EXPERTS * n + ex
            if ex == 0:
                S["eo", q] = dve(lambda e: e.tensor_scalar(acc[:, :], bk[:, :], dnb[:, 0:1], 0.1, ALU.add, ALU.mult),
                                 wait=[t, t_ub, S.get(("accT", n - 1))], sig="v_eo")
                S["acc"] = S["eo", q]
                return
            w = (8 * n + ex - 1) % NW
            S["eo", q] = dve(lambda e: e.scalar_tensor_tensor(
                out=eo_[q % 2][:, :], in0=bk[:, :], scalar=dnb[:, ex:ex + 1], in1=wb_[w][:, :],
                op0=ALU.add, op1=ALU.mult), wait=[t, S["wb", n, ex], S.get(("ea", q - 2))], sig="v_eo")
            S["wbf", w] = S["eo", q]
            S["ea", q] = pool(lambda e: e.tensor_tensor(acc[:, :], acc[:, :], eo_[q % 2][:, :], ALU.add),
                              wait=[S["eo", q], S["acc"]], sig="p_ac")
            S["acc"] = S["ea", q]

        def f_fin(n):
            i, bk, free = bank()
            for b in range(GB):
                t = pe(lambda e, b=b: e.transpose(bk[:, 128 * b:128 * b + 128], acc[:, 128 * b:128 * b + 128], ident),
                       wait=[S["acc"], free], sig="m_fT")
            S["accT", n] = t
            x1 = x1_[n % 2]
            t = dve(lambda e: e.tensor_reduce(am[:, :], bk[:, :].rearrange("p (b h) -> p b h", b=4), AX.X, ALU.max,
                                              apply_absolute_value=True), wait=[t], sig="v_fin")
            t = dve(lambda e: e.tensor_scalar(am[:, :], am[:, :], 1e-6, None, ALU.add), wait=[t], sig="v_fin")
            t = dve(lambda e: e.reciprocal(ar[:, :], am[:, :]), wait=[t], sig="v_fin")
            for b in range(GB):
                tt = dve(lambda e, b=b: e.scalar_tensor_tensor(
                    out=x1[:, b, :], in0=bk[:, 128 * b:128 * b + 128], scalar=ar[:, b:b + 1], in1=x1[:, b, :],
                    op0=ALU.mult, op1=ALU.add), wait=[t], sig="v_fin")
            give(i, tt)
            S["outd", n] = dma(out[GB * n:GB * n + GB].rearrange("b q d -> q b d"), x1[:, :, :], wait=[tt],
                               sig=f"d_out{n % 2}")

        plan = {}

        def at(slot, fn, *args):
            plan.setdefault(slot, []).append((fn, args))

        for n in range(NG):
            o = CH * n
            at(o + 0, a_ctx, n)
            at(o + 0, a_V, n)
            at(o + 0, a_ln, n)
            at(o + 1, a_k, n)
            at(o + 1, a_xhat, n)
            at(o + 2, a_ks, n)
            at(o + 2, a_xT, n)
            at(o + 3, a_xTs, n)
            if n + 1 < NG:
                at(o + 3, load_ctx, n + 1)
            at(o + 4, a_q, n)
            at(o + 6, a_qs, n)
            at(o + 5, a_msk, n)
            at(o + 6, a_kblk, n, 0)
            for b in range(GB):
                p = o + P0 + GAP * b
                if b:
                    at(p - 4, a_kblk, n, b)
                at(p, a_qblk, n, b)
                at(p, a_A, n, b, 0)
                at(p, a_A, n, b, 1)
                at(p + 1, a_A, n, b, 2)
                at(p + 1, a_A, n, b, 3)
                at(p + 2, a_nm, n, b)
                at(p + 3, a_nmT, n, b)
                at(p + 4, a_nmTe, n, b)
                at(p + 4, a_vm, n, b)
                for g in range(4):
                    at(p + 7, a_B, n, b, g)
                at(p + 9, a_PV, n, b)
                at(p + 10, a_norm, n, b)
                at(p + 11, a_wo, n, b)
                at(p + 12, a_x1, n, b)
            p = o + P0 + GAP * 3 + 13
            if n + 1 < NG:
                at(o + 30, load, n + 1)
            at(p, a_ln2, n)
            at(p + 1, a_xn2, n)
            at(p + 2, a_x2T, n)
            at(p + 3, a_x2Ts, n)
            at(p + 4, a_router, n)
            at(p + 5, a_erT, n)
            at(p + 6, a_top1, n)
            at(p + 7, a_top2, n)
            at(p + 8, a_wT, n)
            for ex in range(1, EXPERTS):
                at(o + START + 4 * ex - 1, f_wb, n, ex)
            at(o + START + CH + LAG + 2, f_fin, n)

        for slot in range(START + CH * NG + LAG + 3):
            def ffn(fn, lag):
                k = slot - START - lag
                if 0 <= k < CH * NG:
                    fn(k // CH, k % CH)
            ffn(f_hi, 1)
            ffn(f_up, 0)
            for fn, args in plan.get(slot, []):
                fn(*args)
            ffn(f_gelu, 0)
            ffn(f_lo, 1)
            ffn(f_down, LAG)

        block = ctx.enter_context(nc.Block())

        @block.sync
        def _(e):
            Q.play("sync", e)
            for p in range(2):
                e.wait_ge(Q.sems[f"d_out{p}"], Q.count[f"d_out{p}"])
                e.wait_ge(Q.sems[f"d_wd{p}"], Q.count[f"d_wd{p}"])
            for name in ("d_Qw", "d_Kw"):
                e.wait_ge(Q.sems[name], Q.count[name])

        @block.scalar
        def _(e):
            Q.play("scalar", e)

        @block.vector
        def _(e):
            Q.play("vector", e)

        @block.gpsimd
        def _(e):
            Q.play("gpsimd", e)

        @block.tensor
        def _(e):
            Q.play("tensor", e)


def kernel(**inputs):
    import concourse.bacc as bacc
    from concourse.bass_utils import run_bass_kernel_spmd

    def a(name):
        return np.asarray(inputs[name])

    def c(v):
        return np.ascontiguousarray(v)

    mask = c(a("mask_BxS2_bf0")).view(np.uint8)
    arrays = {
        "x": c(a("x")),
        "ctxT": c(a("ctx_1024").transpose(2, 0, 1).reshape(D, NB * LK)),
        "mask": mask.view(np.int32),
        "maskT": c(mask.T).view(np.int32),
        "wqT": c(a("L0_xattn_wq").T),
        "wkT": c(a("L0_xattn_wk").T),
        "wvT": c(a("L0_xattn_wv").T),
        "woT": c(a("L0_xattn_wo").T),
        "bqT": c(a("L0_xattn_bq").reshape(128, 1)),
        "bkT": c(a("L0_xattn_bk").reshape(128, 1)),
        "bv": c(a("L0_xattn_bv")),
        "bo": c(a("L0_xattn_bo")),
        "gate_w": c(a("L0_ffn_gate_w")),
        "gbias": c(a("L0_ffn_bias").reshape(8, 1)),
        "up_w": c(a("L0_ffn_up_w")),
        "up_bT": c(a("L0_ffn_up_b").reshape(8, 4, 128).transpose(2, 0, 1).reshape(128, 32)),
        "down_w": c(a("L0_ffn_down_w")),
        "down_bT": c(a("L0_ffn_down_b").T),
        "sw_up": c(a("L0_ffn_sw_up")),
        "sb_upT": c(a("L0_ffn_sb_up").reshape(4, 128).T),
        "sw_down": c(a("L0_ffn_sw_down")),
        "sb_downT": c(a("L0_ffn_sb_down").reshape(128, 1)),
        "consts": constants(),
    }
    nc = bacc.Bacc("TRN2", target_bir_lowering=False, num_devices=1)
    feeds, args = {}, []
    for name, v in arrays.items():
        feeds[f"in_{name}"] = v
        args.append(nc.dram_tensor(f"in_{name}", v.shape, mybir.dt.from_np(v.dtype), kind="ExternalInput").ap())
    args.append(nc.dram_tensor("out_0", (NB, LQ, D), F32, kind="ExternalOutput").ap())
    xattn_moe_kernel(nc, *args)
    r = run_bass_kernel_spmd(nc, [feeds], core_ids=[0])
    return r.results[0]["out_0"]
```

```python
from contextlib import ExitStack

import numpy as np

import concourse.bass as bass
from concourse import mybir

F32 = mybir.dt.float32
F32R = mybir.dt.float32r
BF16 = mybir.dt.bfloat16
U8 = mybir.dt.uint8
I32 = mybir.dt.int32
ALU = mybir.AluOpType
ACT = mybir.ActivationFunctionType
AX = mybir.AxisListType

NB, LQ, LK, D = 64, 128, 120, 128
NE, FF = 8, 512
GB = 4
NG = NB // GB
T = GB * LQ
TK = GB * LK
BIG = float(2.0 ** 100)
EPS = 1e-5
SCALE = float(1.0 / np.sqrt(8.0))
EXPERTS = NE + 1
CH = EXPERTS * 4

C_ID, C_CAUS, C_PRIO, C_ONES, C_TRIL, C_N = 0, 128, 248, 280, 408, 536
RG = 5
NPR = 5
NWR = 2
NU = 3
ND = 1

ORDER = "huadgl"
LAG = 4
HL = 1
LL = 1

OQ = 1
OK = -1
OV = -1
XL = 30

Q1 = 1
Q2 = 1
Q3 = 5
Q4 = 9
K1 = 1
K2 = 1

P0 = 13
GAP = 5
G0 = 5
SKEW = 0
KB0 = 6
KB = 5
QB = 1

A1 = 2
A2 = 2
A3 = 2
N1 = 2
N2 = 2
VM = 4
OB = 8
B2 = 0
OP = 10
W0 = 2
W1 = 4
W2 = 4

OL = 4
R0 = 3
R1 = 4
R2 = 4
R3 = 5
R4 = 6
R5 = 6
R6 = 7
OW = 10
WB = -1
FN = 2
SL = 6

WL = 0
WS = 3
WG = 3

HB = 1
HO = 0
LP = ('a_top1',)
HI_ON_DVE = ()

START = P0 + 3 * G0 + SKEW + OP + OL + SL


def constants():
    c = np.zeros((128, C_N), np.float32)
    c[:, C_ID:C_ID + 128] = np.eye(128)
    q, k = np.arange(128)[:, None], np.arange(LK)[None, :]
    c[:, C_CAUS:C_CAUS + LK] = np.where(k > q, -BIG, 0.0)
    c[:, C_PRIO:C_PRIO + 32] = np.tile(8.0 - np.arange(8), 4)
    j = np.arange(4)[:, None]
    m = np.arange(32)[None, :]
    c[:, C_ONES:C_ONES + 128] = (m // 8 == j).astype(np.float32).reshape(-1)
    kk, qq = np.arange(128)[:, None], np.arange(128)[None, :]
    c[:, C_TRIL:C_TRIL + 128] = (kk <= qq)
    return c


class Marks(dict):

    def get(self, key):
        if isinstance(key, tuple) and key[0] not in ("pfree", "ea"):
            return None if key[1] < 0 else self[key]
        return super().get(key)


class Queues:

    def __init__(self, sem):
        self.sem, self.sems, self.count = sem, {}, {}
        self.ops = {n: [] for n in ("tensor", "vector", "scalar", "gpsimd", "sync")}

    def add(self, engine, fn, wait=(), sig=None, by=1):
        token = None
        if sig is not None:
            if sig not in self.sems:
                self.sems[sig], self.count[sig] = self.sem(sig), 0
            self.count[sig] += by
            token = (sig, self.count[sig])
        self.ops[engine].append((fn, [w for w in wait if w is not None], sig, by))
        return token

    def play(self, engine, eng):
        seen = {}
        for fn, wait, sig, by in self.ops[engine]:
            for name, value in wait:
                if seen.get(name, 0) < value:
                    eng.wait_ge(self.sems[name], value)
                    seen[name] = value
            ins = fn(eng)
            if sig is not None:
                ins.then_inc(self.sems[sig], by)


def xattn_moe_kernel(nc, x, ctxT, mask, maskT, wqT, wkT, wvT, woT, bqT, bkT, bv, bo, gate_w, gbias,
                     up_w, up_bT, down_w, down_bT, sw_up, sb_upT, sw_down, sb_downT, consts, out):
    w_dram = nc.dram_tensor("w_scratch", (2, 32, 128), F32, kind="Internal").ap()
    q_dram = nc.dram_tensor("q_scratch", (2, 4, 32, T), F32, kind="Internal").ap()
    n_dram = nc.dram_tensor("n_scratch", (2, 32, 128), F32, kind="Internal").ap()
    m_dram = nc.dram_tensor("m_scratch", (NB, LK), F32, kind="Internal").ap()
    k_dram = nc.dram_tensor("k_scratch", (2, 4, 32, TK), F32, kind="Internal").ap()
    with ExitStack() as ctx:
        def sb(name, shape, dt=F32):
            return ctx.enter_context(nc.sbuf_tensor(name, shape, dt))

        Q = Queues(lambda n: ctx.enter_context(nc.semaphore(n)))

        def pe(fn, wait=(), sig=None):
            return Q.add("tensor", fn, wait, sig)

        def dve(fn, wait=(), sig=None):
            return Q.add("vector", fn, wait, sig)

        def act(fn, wait=(), sig=None):
            return Q.add("scalar", fn, wait, sig)

        def pool(fn, wait=(), sig=None):
            return Q.add("gpsimd", fn, wait, sig)

        def dma(dst, src, wait=(), sig=None, queue="sync"):
            return Q.add(queue, lambda e: e.dma_start(dst, src), wait, sig, 16)

        banks = [ctx.enter_context(nc.psum_tensor(f"bank{i}", [128, 512], F32)) for i in range(8)]
        UPB, DNB, ATT = banks[0:NU], banks[NU:NU + ND], banks[NU + ND:8]

        con = sb("con", [128, C_N])
        ident = con[:, C_ID:C_ID + 128]
        identb = sb("identb", [128, 128], BF16)
        trilb = sb("trilb", [128, 128], BF16)
        onesb = sb("onesb", [128, 128], BF16)
        causb = sb("causb", [128, LK], BF16)
        sc = sb("sc", [128, 1])
        km8 = sb("km8", [NB, LK // 4], I32)
        km = sb("km", [NB, LK], F32R)
        vis = sb("vis", [128, 64], BF16)
        visi = sb("visi", [128, 16], I32)
        visu = visi[:, :].bitcast(U8)
        poison = sb("poison", [128, 64])
        pz = sb("pz", [128, 64])
        pt_ = sb("pt_", [128, 2])
        nhalf = sb("nhalf", [128, 4])

        uph = sb("uph", [128, EXPERTS, FF], F32R)
        upl = sb("upl", [128, EXPERTS, FF], F32R)
        dnh = sb("dnh", [128, EXPERTS, 4, 128], F32R)
        dnl = sb("dnl", [128, EXPERTS, 4, 128], F32R)
        upb = sb("upb", [128, EXPERTS, 4])
        dnb = sb("dnb", [128, EXPERTS])
        wqh = sb("wqh", [128, 128], F32R)
        wql = sb("wql", [128, 128], F32R)
        wkh = sb("wkh", [128, 128], F32R)
        wkl = sb("wkl", [128, 128], F32R)
        wv = sb("wv", [128, 128])
        wo = sb("wo", [128, 128])
        bqk = sb("bqk", [128, 2])
        bvb = sb("bvb", [128, 128])
        bob = sb("bob", [128, 128])
        gwf = sb("gwf", [128, 8])
        gwh = sb("gwh", [128, 8], F32R)
        gwl = sb("gwl", [128, 8], F32R)
        gb = sb("gb", [8, 1])
        ngb = sb("ngb", [8, 1])

        xs_ = [sb(f"x{i}", [128, GB, 128]) for i in range(2)]
        x1_ = [sb(f"x1_{i}", [128, GB, 128]) for i in range(2)]
        xhat = sb("xhat", [128, GB, 128])
        xth = sb("xth", [128, T], F32R)
        xtl = sb("xtl", [128, T], F32R)
        fth_ = [sb(f"fth{i}", [128, T], F32R) for i in range(2)]
        ftl_ = [sb(f"ftl{i}", [128, T], F32R) for i in range(2)]
        cxf = sb("cxf", [128, TK])
        cxh, cxl = xth[:, 0:TK], xtl[:, 0:TK]
        st = sb("st", [128, GB, 6])
        mv = sb("mv", [128, GB, 2])
        ve = sb("ve", [128, GB])
        rstd = sb("rstd", [128, GB])
        st2 = sb("st2", [128, GB, 6])
        mv2 = sb("mv2", [128, GB, 2])
        ve2 = sb("ve2", [128, GB])
        rstd2 = sb("rstd2", [128, GB])
        px = sb("px", [128, T])
        ph = sb("ph", [128, T], F32R)
        pl = sb("pl", [128, T], F32R)
        vv = sb("vv", [128, GB, 128])
        qst = sb("qst", [128, 4, T], F32R)
        kst = sb("kst", [128, 4, TK], F32R)
        kblk = sb("kblk", [128, 4, 4, LK], F32R)
        qblk_ = [sb(f"qblk{i}", [128, 4, 4, 128], F32R) for i in range(2)]
        NP = NPR
        prob = [sb(f"prob{i}", [128, 512]) for i in range(NP)]
        nm = sb("nm", [128, 16])
        nm2 = sb("nm2", [128, 16, 2])
        nmt = sb("nmt", [32, 128], F32R)
        vm_ = [sb(f"vm{i}", [128, 16, 32]) for i in range(2)]
        rsum = sb("rsum", [128, 128])
        oc = sb("oc", [128, 1])
        oT = sb("oT", [128, 128])
        er = sb("er", [8, T])
        s1 = sb("s1", [128, 4, 8])
        s2 = sb("s2", [128, 4, 8])
        eq = sb("eq", [128, 4, 8])
        oh1 = sb("oh1", [128, 4, 8])
        oh2 = sb("oh2", [128, 4, 8])
        m1 = sb("m1", [128, 4])
        m2 = sb("m2", [128, 4])
        pm = sb("pm", [128, 4])
        wgt = sb("wgt", [128, 4, 8])
        wts = sb("wts", [32, 128])
        NW = NWR
        wb_ = [sb(f"wb{i}", [128, T]) for i in range(NW)]
        gf_ = [sb(f"gf{i}", [128, T]) for i in range(2)]
        gh_ = [sb(f"gh{i}", [128, T], F32R) for i in range(RG)]
        gl_ = [sb(f"gl{i}", [128, T], F32R) for i in range(RG)]
        eo_ = [sb(f"eo{i}", [128, T]) for i in range(2)]
        acc = sb("acc", [128, T])
        am = sb("am", [128, 4])
        ar = sb("ar", [128, 4])

        def f(ap):
            return ap.bitcast(F32)

        spare = [(i, None) for i in range(len(ATT))]

        def bank():
            i, last_read = spare.pop(0)
            return i, ATT[i], last_read

        def give(i, last_read):
            spare.append((i, last_read))

        t_con = dma(con[:, :], consts, sig="d_con")
        for dst, src in ((wv[:, :], wvT), (wo[:, :], woT), (gwf[:, :], gate_w), (gb[:, :], gbias),
                         (bvb[:, :], bv.partition_broadcast(128)), (bob[:, :], bo.partition_broadcast(128)),
                         (xhat[:, 0, :], wqT), (xhat[:, 1, :], wkT)):
            t_small = dma(dst, src, sig="d_small")
        t_bias = dma(bqk[:, 0:1], bqT, sig="d_bias")
        t_bias = dma(bqk[:, 1:2], bkT, sig="d_bias")

        t_load = {}

        def load(n):
            assert n < 2 or n - 2 in t_free_x
            p = n % 2
            prev = t_free_x.get(n - 2)
            t_load[n] = dma(xs_[p][:, :, :], x[GB * n:GB * n + GB].rearrange("b q d -> q b d"), wait=[prev], sig=f"d_x{p}")

        def load_ctx(n):
            t_ctx[n] = dma(cxf[:, :], ctxT[:, TK * n:TK * n + TK], wait=[t_cxl.get(n - 1), S.get(("cx", n - 1))], sig="d_ctx")

        S = Marks()
        t_free_x, t_ctx, t_cxl = {}, {}, {}
        load(0)
        load_ctx(0)
        t_vis = dma(visi[0:LK, :], maskT, sig="d_vis")
        t_km8 = dma(km8[:, :], mask, sig="d_km8")
        t_ub = dma(upb[:, 0, :], sb_upT, sig="d_fb")
        t_ub = dma(upb[:, 1:, :], up_bT.rearrange("p (e c) -> p e c", e=8), sig="d_fb")
        t_ub = dma(dnb[:, 0:1], sb_downT, sig="d_fb")
        t_ub = dma(dnb[:, 1:], down_bT, sig="d_fb")

        t_nh = pool(lambda e: e.memset(nhalf[:, :], -0.5), sig="p_nh")
        t_z = pool(lambda e: e.memset(f(kblk[:, :, :, :]), 0.0), sig="p_zk")
        t_zq = None
        for qb in qblk_:
            t_zq = pool(lambda e, qb=qb: e.memset(f(qb[:, :, :, :]), 0.0), sig="p_zq")
        t_zs = pool(lambda e: e.memset(f(qst[:, :, :]), 0.0), sig="p_zs")
        t_zs2 = pool(lambda e: e.memset(f(kst[:, :, :]), 0.0), sig="p_zs")
        t_o = pool(lambda e: e.memset(f(ph[0:4, :]), 1.0), sig="p_zs")
        for r in (24, 25):
            t_tail = dma(f(kst[r:128:32, :, :]), f(ph[0:4, 0:TK]).unsqueeze(1).to_broadcast([4, 4, TK]),
                         wait=[t_zs2, t_o], sig="d_tail")
        t_tail = dma(f(qst[26:128:32, :, :]), f(ph[0:4, :]).unsqueeze(1).to_broadcast([4, 4, T]),
                     wait=[t_zs, t_o], sig="d_tail")
        for qb in qblk_:
            t_tail = dma(f(qb[26:27, :, :, :]).rearrange("p g j q -> p g (j q)"),
                         f(ph[0:1, :]).unsqueeze(1).to_broadcast([1, 4, T]), wait=[t_zq, t_o], sig="d_tail")
        S["pd"] = t_tail
        for v in vm_:
            t_zv = pool(lambda e, v=v: e.memset(v[:, :, :], 0.0), sig="p_zv")
        for pr in prob:
            t_zp = pool(lambda e, pr=pr: e.memset(pr[:, :], 0.0), sig="p_zp")
        t_one = pool(lambda e: e.memset(onesb[:, :], 1.0), sig="p_one")

        for src, wh, wl in ((0, wqh, wql), (1, wkh, wkl)):
            t = dve(lambda e, wh=wh, src=src: e.tensor_copy(wh[:, :], xhat[:, src, :]), wait=[t_small], sig="v_wh")
            t_w = dve(lambda e, wh=wh, wl=wl, src=src: e.tensor_tensor(wl[:, :], xhat[:, src, :], f(wh[:, :]),
                                                                       ALU.subtract), wait=[t], sig="v_wl")
        t = dve(lambda e: e.tensor_copy(gwh[:, :], gwf[:, :]), sig="v_gw")
        dve(lambda e: e.tensor_tensor(gwl[:, :], gwf[:, :], f(gwh[:, :]), ALU.subtract), wait=[t], sig="v_gw")
        t_gw = dve(lambda e: e.tensor_scalar(ngb[:, :], gb[:, :], -1.0, None, ALU.mult), sig="v_gw")
        dve(lambda e: e.tensor_copy(identb[:, :], ident), wait=[t_con], sig="v_id")
        dve(lambda e: e.tensor_copy(causb[:, :], con[:, C_CAUS:C_CAUS + LK]), sig="v_id")
        t_id = dve(lambda e: e.tensor_copy(trilb[:, :], con[:, C_TRIL:C_TRIL + 128]), sig="v_id")

        t = dve(lambda e: e.tensor_scalar(km[:, :], km8[:, :].bitcast(U8), -BIG, None, ALU.mult), wait=[t_km8], sig="v_km")
        t_km = dma(m_dram, f(km[:, :]), wait=[t], sig="d_km")

        t = dve(lambda e: e.tensor_scalar(vis[0:LK, :], visu[0:LK, :], -1.0, 1.0, ALU.mult, ALU.add),
                wait=[t_vis], sig="v_vis")
        i, bk, free = bank()
        pe(lambda e, bk=bk: e.matmul(bk[:, 0:64], trilb[0:LK, :], vis[0:LK, :], start=True, stop=True),
           wait=[t, t_id, t_one])
        t = pe(lambda e, bk=bk: e.matmul(bk[:, 64:128], onesb[0:LK, :], vis[0:LK, :], start=True, stop=True,
                                         skip_group_check=True), sig="m_vis")
        dve(lambda e, bk=bk: e.tensor_reduce(pt_[:, 0:1], bk[:, 64:128], AX.X, ALU.add), wait=[t], sig="v_poi")
        t = dve(lambda e, bk=bk: e.tensor_scalar(pz[:, :], bk[:, 0:64], 0.0, 3e38, ALU.is_equal, ALU.mult), sig="v_poi")
        give(i, t)
        t = dve(lambda e: e.tensor_scalar(pt_[:, 1:2], pt_[:, 0:1], 0.0, None, ALU.is_gt), wait=[t], sig="v_poi")
        dve(lambda e: e.tensor_scalar(pt_[:, 0:1], pt_[:, 1:2], -1.0, 1.0, ALU.mult, ALU.add), wait=[t], sig="v_poi")
        t_cap = dve(lambda e: e.tensor_scalar(sc[:, :], pt_[:, 1:2], SCALE, None, ALU.mult), wait=[t], sig="v_poi")
        t = dve(lambda e: e.tensor_scalar(poison[:, :], pz[:, :], pt_[:, 1:2], 10.0, ALU.mult, ALU.mult),
                wait=[t], sig="v_poi")
        t_poison = dve(lambda e: e.tensor_tensor(pz[:, :], poison[:, :], poison[:, :], ALU.subtract),
                       wait=[t], sig="v_poi")

        stage = [*gf_, *eo_, *wb_, acc]
        staged, stage_free = {}, {}
        t_fw = {}

        def w_load(k):
            ex, what = divmod(k, 2)
            s = stage[k % len(stage)]
            if what == 0:
                src, dst = sw_up if ex == 0 else up_w[ex - 1], s[:, :]
            else:
                src = (sw_down if ex == 0 else down_w[ex - 1]).rearrange("(c p) h -> p c h", p=128)
                dst = s[:, :].rearrange("p (c h) -> p c h", c=4)
            staged[k] = dma(dst, src, wait=[stage_free.get(k - len(stage))], sig=f"d_w{k % len(stage)}")

        def w_split(k):
            ex, what = divmod(k, 2)
            s = stage[k % len(stage)]
            if what == 0:
                h, l = uph[:, ex, :], upl[:, ex, :]
            else:
                h = dnh[:, ex, :, :].rearrange("p c h -> p (c h)")
                l = dnl[:, ex, :, :].rearrange("p c h -> p (c h)")
            ta = act(lambda e: e.activation(h, s[:, :], ACT.Copy), wait=[staged[k]], sig="a_wh")
            tp = pool(lambda e: e.tensor_tensor(l, s[:, :], f(h), ALU.subtract), wait=[ta, staged[k]], sig="p_wl")
            stage_free[k] = tp
            t_fw[ex] = tp
            if k and k - 1 + len(stage) < 2 * EXPERTS:
                w_load(k - 1 + len(stage))

        def ln_a(n, src, stats, agg, v, wait, tag):
            for b in range(GB):
                t = dve(lambda e, b=b: e.bn_stats(stats[:, b, :], src[:, b, :]), wait=wait, sig=f"v_st{tag}")
            for b in range(GB):
                t = dve(lambda e, b=b: e.bn_aggr(agg[:, b, :], stats[:, b, :]), wait=[t], sig=f"v_ag{tag}")
            return dve(lambda e: e.tensor_scalar(v[:, :], agg[:, :, 1], EPS, None, ALU.add),
                       wait=[t], sig=f"v_ve{tag}")

        def a_ln(n):
            xt = xs_[n % 2]
            t = ln_a(n, xt, st, mv, ve, [t_load[n], t_w], "1")
            S["rs", n] = pool(lambda e: e.tensor_tensor(rstd[:, :], ve[:, :], nhalf[:, :], ALU.pow),
                              wait=[t, t_nh, S.get(("xhat", n - 1))], sig="p_rs1")

        def a_ctx(n):
            t = act(lambda e: e.activation(cxh, cxf[:, :], ACT.Copy), wait=[t_ctx[n], S.get("xa")],
                    sig="a_ch")
            S["halves"] = "K", n
            S["cx", n] = dve(lambda e: e.tensor_tensor(cxl, cxf[:, :], f(cxh), ALU.subtract), wait=[t], sig="v_cl")

        def a_xhat(n):
            xt = xs_[n % 2]
            for b in range(GB):
                t = dve(lambda e, b=b: e.tensor_scalar(
                    xhat[:, b, :], xt[:, b, :], mv[:, b, 0:1], rstd[:, b:b + 1], ALU.subtract, ALU.mult),
                    wait=[S["rs", n], S.get("xhf")], sig="v_xh")
            S["owner"] = "x", n
            S["xhat", n] = t
            S["xb", n] = pool(lambda e: e.tensor_tensor(
                xt[:, :, :], xt[:, :, :], bob[:, :].unsqueeze(1).to_broadcast([128, GB, 128]), ALU.add),
                wait=[t, t_small], sig="p_xb")

        def tr4(src, wait, sig):
            i, bk, free = bank()
            for b in range(GB):
                t = pe(lambda e, b=b: e.transpose(bk[:, 128 * b:128 * b + 128], src[:, b, :], ident),
                       wait=[*wait, free], sig=sig)
            return i, bk, t

        def split(n, i, bk, t, hi, lo, wait, tag):
            th = act(lambda e: e.activation(hi[:, :], bk[:, :], ACT.Copy), wait=[t, *wait], sig=f"a_{tag}")
            tl = dve(lambda e: e.tensor_tensor(lo[:, :], bk[:, :], f(hi[:, :]), ALU.subtract),
                     wait=[th, *wait], sig=f"v_{tag}")
            give(i, tl)
            return tl

        def a_xT(n):
            assert S["owner"] == ("x", n)
            S["xT", n] = i, bk, t = tr4(xhat, [S["xhat", n], t_con], "m_xT")
            S["xhf"] = t

        def a_xTs(n):
            i, bk, t = S["xT", n]
            S["halves"] = "Q", n
            S["xt", n] = split(n, i, bk, t, xth, xtl, [S.get("xa")], "xt")

        def project(n, wh, wl, ch, cl, N, wait, col, dram, dst, free_dst, tag):
            assert S["halves"] == (tag, n)
            i, bk, free = bank()
            pe(lambda e: e.matmul(bk[:, 0:N], wh[:, :], ch, start=True, stop=False), wait=[*wait, t_w, free])
            pe(lambda e: e.matmul(bk[:, 0:N], wh[:, :], cl, start=False, stop=False))
            S["xa"] = t = pe(lambda e: e.matmul(bk[:, 0:N], wl[:, :], ch, start=False, stop=True),
                                     sig=f"m_{tag}")
            ta = act(lambda e: e.activation(px[:, 0:N], bk[:, 0:N], ACT.Identity, bias=bqk[:, col:col + 1]),
                     wait=[t, t_bias, S.get("px")], sig=f"a_{tag}")
            give(i, ta)
            th = dve(lambda e: e.tensor_copy(ph[:, 0:N], px[:, 0:N]), wait=[ta, S.get("pd")], sig=f"v_{tag}h")
            S["px"] = tl = dve(lambda e: e.tensor_tensor(pl[:, 0:N], px[:, 0:N], f(ph[:, 0:N]), ALU.subtract),
                               wait=[th, S.get("pd")], sig=f"v_{tag}l")
            dma(dram[0].rearrange("g r t -> (g r) t"), f(ph[:, 0:N]), wait=[th, S.get(("stk" + tag, n - 1))], sig=f"d_{tag}w")
            td = dma(dram[1].rearrange("g r t -> (g r) t"), f(pl[:, 0:N]), wait=[tl], sig=f"d_{tag}w")
            S["pd"] = td
            S["w" + tag, n] = td

        def stack(n, dram, parts, dst, free_dst, tag):
            for j in range(4):
                for part, hl in enumerate(parts):
                    r = 32 * j + 8 * part
                    t = dma(f(dst[r:r + 8, :, :]), dram[hl, :, 8 * j:8 * j + 8, :].rearrange("g d t -> d g t"),
                            wait=[S["w" + tag, n], *free_dst, t_tail], sig=f"d_{tag}s")
            if tag == "K":
                t = dma(f(dst[26:128:32, :, :]), m_dram[GB * n:GB * n + GB, :].rearrange("b k -> (b k)").unsqueeze(0)
                        .unsqueeze(0).to_broadcast([4, 4, TK]), wait=[t_km, *free_dst, t_tail], sig="d_Ks")
            S["stk" + tag, n] = t

        def a_k(n):
            project(n, wkh, wkl, cxh, cxl, TK, [S["cx", n]], 1, k_dram, kst, None, "K")

        def a_ks(n):
            stack(n, k_dram, (0, 1, 0), kst, [S.get(("Bd", n - 1, 3)), S.get(("kbl", n - 1))], "K")

        def a_q(n):
            project(n, wqh, wql, xth[:, :], xtl[:, :], T, [S["xt", n]], 0, q_dram, qst, None, "Q")

        def a_qs(n):
            stack(n, q_dram, (0, 0, 1), qst, [S.get(("Aend", n - 1)), S.get(("qcopy", n - 1))], "Q")

        def a_kblk(n, b):
            S.get(("A4", prev(n, b)))
            t = None
            for j in range(4):
                t = dma(f(kblk[32 * j:32 * j + 32, :, j, :]), f(kst[32 * j:32 * j + 32, :, LK * b:LK * b + LK]),
                        wait=[S["stkK", n], S.get(("Ad", prev(n, b))), t_z, t_tail], sig="d_kb")
            S["kb", n, b] = t
            S["kbl", n] = t

        def prev(n, b, back=1):
            return GB * n + b - back

        def a_qblk(n, b):
            q = (GB * n + b) % 2
            for j in range(4):
                t = dma(f(qblk_[q][32 * j:32 * j + 24, :, j, :]), f(qst[32 * j:32 * j + 24, :, 128 * b:128 * b + 128]),
                        wait=[S["stkQ", n], S.get(("Bdone", prev(n, b, 2))), t_zq], sig=f"d_qb{q}")
            S["qcopy", n] = t

        def a_A(n, b, g):
            i, bk, free = bank()
            pe(lambda e: e.matmul(bk[:, 0:480], qst[:, g, 128 * b:128 * b + 128],
                                  kblk[:, g, :, :].rearrange("p a b -> p (a b)"), start=True, stop=False),
               wait=[S["kb", n, b], S["stkQ", n], t_zs, free])
            t = pe(lambda e: e.matmul(bk[:, 0:480].rearrange("p (j k) -> p j k", j=4), identb[:, :],
                                      causb[:, :].unsqueeze(1).to_broadcast([128, 4, LK]), start=False, stop=True),
                   wait=[t_id], sig="m_A")
            tm = dve(lambda e: e.tensor_reduce(nm[:, 4 * g:4 * g + 4], bk[:, 0:480].rearrange("p (j k) -> p j k", j=4),
                                               AX.X, ALU.max, negate=True),
                     wait=[t, S.get("nm_free")], sig="v_mx")
            give(i, tm)
            S["mx", n, b] = tm
            S["Ad", GB * n + b] = t
            S["Agroups", n, b] = dict.get(S, ("Agroups", n, b), 0) + 1
            if S["Agroups", n, b] == 4:
                S["A4", GB * n + b] = t
            if b == 3:
                S["Aend", n] = t

        def a_nm(n, b):
            assert S["Agroups", n, b] == 4
            t = dve(lambda e: e.tensor_copy(nm2[:, :, 0].bitcast(F32R), nm[:, :]), wait=[S["mx", n, b], S.get("nmT_read")],
                    sig="v_nm")
            S["nm", n, b] = dve(lambda e: e.tensor_tensor(nm2[:, :, 1], nm[:, :], nm2[:, :, 0], ALU.subtract),
                                wait=[t], sig="v_nm")
            S["nm_free"] = S["nm", n, b]

        def a_nmT(n, b):
            i, bk, free = bank()
            S["nmT_read"] = t = pe(lambda e: e.transpose(bk[0:32, 0:128], nm2[:, :, :].rearrange("p a b -> p (a b)"), ident),
                                   wait=[S["nm", n, b], free], sig="m_nT")
            S["nmT", n, b] = i, bk, t

        def a_nmTe(n, b):
            i, bk, t = S["nmT", n, b]
            te = dve(lambda e: e.tensor_copy(nmt[:, :], bk[0:32, 0:128]), wait=[t, S.get("nmt_free")], sig="v_nT")
            give(i, te)
            q = (GB * n + b) % 2
            t = dma(n_dram[q], f(nmt[:, :]), wait=[te, S.get(("qb", *divmod(prev(n, b, 2), GB)))], sig=f"d_nw{q}")
            S["nmt_free"] = t
            for j in range(4):
                t = dma(f(qblk_[q][32 * j + 24:32 * j + 26, :, j, :]),
                        n_dram[q].rearrange("(g j r) q -> j r g q", g=4, j=4)[j],
                        wait=[S["nmt_free"], S.get(("Bdone", prev(n, b, 2))), t_zq], sig=f"d_qb{q}")
            S["qb", n, b] = t

        def a_V(n):
            i, bk, free = bank()
            for b in range(GB):
                t = pe(lambda e, b=b: e.matmul(bk[0:LK, 128 * b:128 * b + 128], cxf[:, LK * b:LK * b + LK], wv[:, :],
                                               start=True, stop=True, skip_group_check=True),
                       wait=[t_ctx[n], t_small, free], sig="m_V")
            S["Vp", n] = t
            t_cxl[n] = t
            te = dve(lambda e: e.tensor_tensor(
                vv[0:LK, :, :], bk[0:LK, :].rearrange("p (b d) -> p b d", b=4),
                bvb[0:LK, :].unsqueeze(1).to_broadcast([LK, GB, 128]), ALU.add),
                wait=[t, t_small, S.get(("vm", n - 1, 3))], sig="v_V")
            give(i, te)
            S["V", n] = te

        def a_vm(n, b):
            vm = vm_[(GB * n + b) % 2]
            for j in range(4):
                t = pool(lambda e, j=j: e.tensor_copy(
                    vm[0:LK, :, :].rearrange("p (g j) m -> p g j m", g=4)[:, :, j, 8 * j:8 * j + 8],
                    vv[0:LK, b, :].rearrange("p (g j d) -> p g j d", g=4, j=4)[:, :, j, :]),
                    wait=[S["V", n], t_zv, S.get(("PVd", prev(n, b, 2)))], sig="p_vm")
            S["vm", n, b] = t

        def a_B(n, b, g):
            i, bk, free = bank()
            q = (GB * n + b) % 2
            S.get(("PVd", prev(n, b)))
            s = (4 * (GB * n + b) + g) % NP
            t = pe(lambda e: e.matmul(bk[0:LK, :], kst[:, g, LK * b:LK * b + LK],
                                      qblk_[q][:, g, :, :].rearrange("p a b -> p (a b)"), start=True, stop=True),
                   wait=[S["qb", n, b], free], sig="m_B")
            S["Bgroups", n, b] = dict.get(S, ("Bgroups", n, b), 0) + 1
            if S["Bgroups", n, b] == 4:
                S["Bdone", GB * n + b] = t
            if S["Bgroups", n, b] == 4:
                S["Bd", n, b] = t
            te = act(lambda e: e.activation(prob[s][0:LK, :], bk[0:LK, :], ACT.Exp, scale=sc[0:LK, 0:1]),
                     wait=[t, S.get(("pfree", s)), t_cap, t_zp], sig="a_ex")
            give(i, te)
            pv = prob[s][0:LK, :].rearrange("p (j q) -> p j q", j=4)
            S["P", n, b, g] = pool(lambda e: e.affine_select(
                out=pv, in_=pv, compare_op=ALU.is_ge, fill=0.0, base=0, pattern=[[0, 4], [1, 128]],
                channel_multiplier=-1), wait=[te], sig="p_cut")

        ones32 = con[:, C_ONES:C_ONES + 128].rearrange("p (j m) -> p j m", j=4)

        def a_PV(n, b):
            i, bk, free = bank()
            vm = vm_[(GB * n + b) % 2]
            for half in range(2):
                for j in range(4):
                    for g in range(4):
                        s = (4 * (GB * n + b) + g) % NP
                        w = vm[:, 4 * g + j, :] if half == 0 else ones32[:, j, :]
                        t = pe(lambda e, g=g, j=j, s=s, w=w, half=half: e.matmul(
                            bk[32 * g:32 * g + 32, 128 * half:128 * half + 128], w,
                            prob[s][:, 128 * j:128 * j + 128], start=(j == 0), stop=(j == 3), skip_group_check=True),
                            wait=[S["P", n, b, g], S["vm", n, b], free, t_zp],
                            sig="m_PV")
                        if half == 1 and j == 3:
                            S["pfree", s] = t
            S["PVd", GB * n + b] = t
            S["PV", n, b] = i, bk, t

        def a_norm(n, b):
            i, bk, t = S["PV", n, b]
            tr = dve(lambda e: e.reciprocal(rsum[:, :], bk[:, 128:256]), wait=[t, S.get("oT")], sig="v_rs")
            to = dve(lambda e: e.tensor_tensor(rsum[:, :], bk[:, 0:128], rsum[:, :], ALU.mult),
                     wait=[tr], sig="v_oT")
            give(i, to)
            tc = dve(lambda e: e.tensor_tensor(oc[:, :], rsum[:, 127:128], pt_[:, 0:1], ALU.mult), wait=[to, t_cap],
                     sig="v_oT")
            to = dve(lambda e: e.tensor_scalar(oT[:, :], rsum[:, :], pt_[:, 1:2], oc[:, 0:1], ALU.mult, ALU.add),
                     wait=[tc, S.get("Wo")], sig="v_oT")
            S["oT"] = to
            S["oTof"] = n, b

        def a_wo(n, b):
            assert S["oTof"] == (n, b)
            i, bk, free = bank()
            t = pe(lambda e: e.matmul(bk[:, 0:128], oT[:, :], wo[:, :], start=True, stop=True),
                   wait=[S["oT"], t_small, free], sig="m_wo")
            S["Wo"] = t
            S["wo", n, b] = i, bk, t

        def a_x1(n, b):
            i, bk, t = S["wo", n, b]
            xt, x1 = xs_[n % 2], x1_[n % 2]
            t = dve(lambda e: e.scalar_tensor_tensor(
                out=x1[:, b, :], in0=bk[:, 0:128], scalar=pz[:, GB * n + b:GB * n + b + 1], in1=xt[:, b, :],
                op0=ALU.add, op1=ALU.add), wait=[t, S["xb", n], t_poison, S.get(("outd", n - 2))], sig="v_x1")
            give(i, t)
            S["x1", n] = t
            if b == 3:
                t_free_x[n] = t

        def a_ln2(n):
            t = ln_a(n, x1_[n % 2], st2, mv2, ve2, [S["x1", n]], "2")
            S["rs2", n] = pool(lambda e: e.tensor_tensor(rstd2[:, :], ve2[:, :], nhalf[:, :], ALU.pow),
                               wait=[t, S.get(("xh2", n - 1))], sig="p_rs2")

        def a_xn2(n):
            x1 = x1_[n % 2]
            for b in range(GB):
                t = dve(lambda e, b=b: e.tensor_scalar(
                    xhat[:, b, :], x1[:, b, :], mv2[:, b, 0:1], rstd2[:, b:b + 1], ALU.subtract, ALU.mult),
                    wait=[S["rs2", n], S["xhf"]], sig="v_xh2")
            S["owner"] = "x2", n
            S["xh2", n] = t

        def a_x2T(n):
            assert S["owner"] == ("x2", n)
            S["x2T", n] = i, bk, t = tr4(xhat, [S["xh2", n]], "m_x2T")
            S["xhf"] = t

        def a_x2Ts(n):
            i, bk, t = S["x2T", n]
            S["ft", n] = split(n, i, bk, t, fth_[n % 2], ftl_[n % 2],
                               [S.get(("upd", n - 2)), S.get(("rt", n - 2))], "ft")

        def a_router(n):
            i, bk, free = bank()
            h, l = fth_[n % 2], ftl_[n % 2]
            pe(lambda e: e.matmul(bk[0:8, :], gwh[:, :], h[:, :], start=True, stop=False),
               wait=[S["ft", n], t_gw, free])
            pe(lambda e: e.matmul(bk[0:8, :], gwl[:, :], h[:, :], start=False, stop=False))
            t = pe(lambda e: e.matmul(bk[0:8, :], gwh[:, :], l[:, :], start=False, stop=True), sig="m_rt")
            S["rt", n] = t
            S["er", n] = act(lambda e: e.activation(er[:, :], bk[0:8, :], ACT.Exp, scale=-1.0, bias=ngb[:, 0:1]),
                             wait=[t, t_gw, S.get(("erT", n - 1))], sig="a_er")
            give(i, S["er", n])

        def a_erT(n):
            i, bk, free = bank()
            for b in range(GB):
                t = pe(lambda e, b=b: e.transpose(bk[:, 8 * b:8 * b + 8], er[:, 128 * b:128 * b + 128], ident[0:8, 0:8]),
                       wait=[S["er", n], free], sig="m_eT")
            S["erT", n] = t
            t = dve(lambda e: e.tensor_scalar(s2[:, :, :], bk[:, 0:32].rearrange("p (b e) -> p b e", b=4), 1.0, None,
                                              ALU.add), wait=[t], sig="v_top")
            give(i, t)
            S["top"] = dve(lambda e: e.reciprocal(s1[:, :, :], s2[:, :, :]), wait=[t], sig="v_top")

        prio = con[:, C_PRIO:C_PRIO + 32].rearrange("p (b e) -> p b e", b=4)

        def bc(a):
            return a[:, :].unsqueeze(2).to_broadcast([128, 4, 8])

        def first(src, m, oh):
            def step(fn):
                S["top"] = dve(fn, wait=[S["top"]], sig="v_top")
            step(lambda e: e.tensor_reduce(m[:, :], src[:, :, :], AX.X, ALU.max))
            step(lambda e: e.tensor_tensor(eq[:, :, :], src[:, :, :], bc(m), ALU.is_equal))
            step(lambda e: e.tensor_tensor(eq[:, :, :], eq[:, :, :], prio, ALU.mult))
            step(lambda e: e.tensor_reduce(pm[:, :], eq[:, :, :], AX.X, ALU.max))
            step(lambda e: e.tensor_tensor(oh[:, :, :], eq[:, :, :], bc(pm), ALU.is_equal))

        def a_top1(n):
            first(s1, m1, oh1)
            S["top"] = dve(lambda e: e.scalar_tensor_tensor(
                out=s2[:, :, :], in0=oh1[:, :, :], scalar=-4.0, in1=s1[:, :, :], op0=ALU.mult, op1=ALU.add),
                wait=[S["top"]], sig="v_top")

        def a_top2(n):
            first(s2, m2, oh2)

            def step(fn, wait=()):
                S["top"] = dve(fn, wait=[S["top"], *wait], sig="v_top")
            step(lambda e: e.tensor_tensor(oh1[:, :, :], oh1[:, :, :], oh2[:, :, :], ALU.add))
            step(lambda e: e.tensor_tensor(s1[:, :, :], s1[:, :, :], oh1[:, :, :], ALU.mult))
            step(lambda e: e.scalar_tensor_tensor(out=m1[:, :], in0=m1[:, :], scalar=1e-6, in1=m2[:, :],
                                                  op0=ALU.add, op1=ALU.add))
            step(lambda e: e.reciprocal(m2[:, :], m1[:, :]))
            step(lambda e: e.scalar_tensor_tensor(out=wgt[:, :, :], in0=s1[:, :, :], scalar=0.1, in1=bc(m2),
                                                  op0=ALU.mult, op1=ALU.mult), wait=[S.get("wT")])

        def a_wT(n):
            i, bk, free = bank()
            S["wT"] = t = pe(lambda e: e.transpose(bk[0:32, 0:128], wgt[:, :, :].rearrange("p b e -> p (b e)"), ident),
                             wait=[S["top"], free], sig="m_wT")
            t = dve(lambda e: e.tensor_copy(wts[:, :], bk[0:32, 0:128]), wait=[t, S.get(("wd", n - 1))], sig="v_wT")
            give(i, t)
            S["wd", n] = dma(w_dram[n % 2], wts[:, :], wait=[t, S.get(("wbl", n - 2))], sig=f"d_wd{n % 2}")

        def f_wb(n, ex):
            m = (8 * n + ex - 1) % NW
            S["wb", n, ex] = dma(
                wb_[m][:, :].rearrange("p (b q) -> p b q", b=4),
                w_dram[n % 2].rearrange("(b e) q -> e b q", b=4)[ex - 1].partition_broadcast(128),
                wait=[S["wd", n], S.get(("wbf", 8 * n + ex - 1 - NW)), t_fw[EXPERTS - 1]], sig=f"d_wb{m}")
            S["wbl", n] = S["wb", n, ex]

        plan = {}

        def f_up(n, c):
            ex, cc = c // 4, c % 4
            k = CH * n + c
            bk = UPB[k % NU]
            h, l = fth_[n % 2], ftl_[n % 2]
            cols = slice(128 * cc, 128 * cc + 128)
            pe(lambda e: e.matmul(bk[:, :], uph[:, ex, cols], h[:, :], start=True, stop=False),
               wait=[S["ft", n], t_fw[ex], S.get(("gelu", k - NU))])
            pe(lambda e: e.matmul(bk[:, :], uph[:, ex, cols], l[:, :], start=False, stop=False))
            S["up", k] = pe(lambda e: e.matmul(bk[:, :], upl[:, ex, cols], h[:, :], start=False, stop=True), sig="m_up")
            if c == CH - 1:
                S["upd", n] = S["up", k]

        def f_gelu(n, c):
            ex, cc = c // 4, c % 4
            k = CH * n + c
            S["gelu", k] = act(lambda e: e.activation(gf_[k % 2][:, :], UPB[k % NU][:, :], ACT.Gelu,
                                                      bias=upb[:, ex, cc:cc + 1]),
                               wait=[S["up", k], t_ub, S.get(("lo", k - 2)), t_fw[EXPERTS - 1]], sig="a_ge")

        def beside(first, count, names):
            return any(fn.__name__ in names for i in range(count) for fn, _ in plan.get(S["slot"] - first - i, []))

        def f_hi(n, c):
            k = CH * n + c
            wait = [S["gelu", k], S.get(("dn", k - RG))]
            if k % 6 in HI_ON_DVE or beside(HO, HB, ("a_B",)):
                S["hi", k] = dve(lambda e: e.tensor_copy(gh_[k % RG][:, :], gf_[k % 2][:, :]), wait=wait, sig="v_gh")
            else:
                S["hi", k] = act(lambda e: e.activation(gh_[k % RG][:, :], gf_[k % 2][:, :], ACT.Copy), wait=wait,
                                 sig="a_gh")

        def f_lo(n, c):
            k = CH * n + c
            engine, sig = (pool, "p_gl") if beside(0, 1, LP) else (dve, "v_gl")
            S["lo", k] = engine(lambda e: e.tensor_tensor(gl_[k % RG][:, :], gf_[k % 2][:, :], f(gh_[k % RG][:, :]),
                                                       ALU.subtract),
                             wait=[S["hi", k], S.get(("dn", k - RG))], sig=sig)

        def f_down(n, c):
            ex, cc = c // 4, c % 4
            k = CH * n + c
            q = EXPERTS * n + ex
            bk = DNB[q % ND]
            h, l = gh_[k % RG], gl_[k % RG]
            pe(lambda e: e.matmul(bk[:, :], dnh[:, ex, cc, :], h[:, :], start=(cc == 0), stop=False),
               wait=[S["hi", k], S["lo", k], S.get(("eo", q - ND))])
            pe(lambda e: e.matmul(bk[:, :], dnl[:, ex, cc, :], h[:, :], start=False, stop=False))
            S["dn", k] = t = pe(lambda e: e.matmul(bk[:, :], dnh[:, ex, cc, :], l[:, :], start=False, stop=(cc == 3)),
                                sig="m_dn")
            if cc < 3:
                return
            if ex == 0:
                S["eo", q] = dve(lambda e: e.tensor_scalar(acc[:, :], bk[:, :], dnb[:, 0:1], 0.1, ALU.add, ALU.mult),
                                 wait=[t, t_ub, S.get(("accT", n - 1))], sig="v_eo")
                S["acc"] = S["eo", q]
                return
            w = (8 * n + ex - 1) % NW
            S["eo", q] = dve(lambda e: e.scalar_tensor_tensor(
                out=eo_[q % 2][:, :], in0=bk[:, :], scalar=dnb[:, ex:ex + 1], in1=wb_[w][:, :],
                op0=ALU.add, op1=ALU.mult), wait=[t, S["wb", n, ex], S.get(("ea", q - 2))], sig="v_eo")
            S["wbf", 8 * n + ex - 1] = S["eo", q]
            S["ea", q] = pool(lambda e: e.tensor_tensor(acc[:, :], acc[:, :], eo_[q % 2][:, :], ALU.add),
                              wait=[S["eo", q], S["acc"]], sig="p_ac")
            S["acc"] = S["ea", q]

        def f_fin(n):
            i, bk, free = bank()
            for b in range(GB):
                t = pe(lambda e, b=b: e.transpose(bk[:, 128 * b:128 * b + 128], acc[:, 128 * b:128 * b + 128], ident),
                       wait=[S["acc"], free], sig="m_fT")
            S["accT", n] = t
            x1 = x1_[n % 2]
            t = dve(lambda e: e.tensor_reduce(am[:, :], bk[:, :].rearrange("p (b h) -> p b h", b=4), AX.X, ALU.max,
                                              apply_absolute_value=True), wait=[t], sig="v_fin")
            t = dve(lambda e: e.tensor_scalar(am[:, :], am[:, :], 1e-6, None, ALU.add), wait=[t], sig="v_fin")
            t = dve(lambda e: e.reciprocal(ar[:, :], am[:, :]), wait=[t], sig="v_fin")
            for b in range(GB):
                tt = dve(lambda e, b=b: e.scalar_tensor_tensor(
                    out=x1[:, b, :], in0=bk[:, 128 * b:128 * b + 128], scalar=ar[:, b:b + 1], in1=x1[:, b, :],
                    op0=ALU.mult, op1=ALU.add), wait=[t], sig="v_fin")
            give(i, tt)
            S["outd", n] = dma(out[GB * n:GB * n + GB].rearrange("b q d -> q b d"), x1[:, :, :], wait=[tt],
                               sig=f"d_out{n % 2}")


        def at(slot, fn, *args):
            plan.setdefault(slot, []).append((fn, args))

        for k in range(len(stage)):
            at(WL, w_load, k)
        for k in range(2 * EXPERTS):
            at(WS + k * WG // 2, w_split, k)
        for n in range(NG):
            gap = GAP if n else G0
            o = CH * n + (3 * (G0 - GAP) if n else 0)
            at(o + OQ - 1, a_ln, n)
            at(o + OQ, a_xhat, n)
            at(o + OQ + Q1, a_xT, n)
            at(o + OQ + Q2, a_xTs, n)
            at(o + OQ + Q3, a_q, n)
            at(o + OQ + Q4, a_qs, n)
            at(o + OK, a_ctx, n)
            at(o + OV, a_V, n)
            if n + 1 < NG:
                at(o + OV + 1, load_ctx, n + 1)
            at(o + OK + K1, a_k, n)
            at(o + OK + K2, a_ks, n)
            at(o + P0 - KB0, a_kblk, n, 0)
            for b in range(GB):
                p = o + P0 + gap * b + (SKEW if b == 3 else 0)
                if b:
                    at(max(p - KB, p - gap + max(A1, A2, A3)), a_kblk, n, b)
                at(p - QB, a_qblk, n, b)
                at(p, a_A, n, b, 0)
                at(p + A1, a_A, n, b, 1)
                at(p + A2, a_A, n, b, 2)
                at(p + A3, a_A, n, b, 3)
                at(p + A3 + 1, a_nm, n, b)
                at(p + A3 + N1, a_nmT, n, b)
                at(p + A3 + N2, a_nmTe, n, b)
                at(p + VM, a_vm, n, b)
                at(p + OB, a_B, n, b, 0)
                at(p + OB, a_B, n, b, 1)
                at(p + OB + B2, a_B, n, b, 2)
                at(p + OB + B2, a_B, n, b, 3)
                at(p + OP, a_PV, n, b)
                at(p + OP + W0, a_norm, n, b)
                at(p + OP + W1, a_wo, n, b)
                at(p + OP + W2, a_x1, n, b)
            p = o + P0 + gap * 3 + SKEW + OP + OL
            if n:
                at(o - CH + XL, load, n)
            at(p, a_ln2, n)
            at(p + R0, a_xn2, n)
            at(p + R1, a_x2T, n)
            at(p + R2, a_x2Ts, n)
            at(p + R3, a_router, n)
            at(p + R4, a_erT, n)
            at(p + R5, a_top1, n)
            at(p + R6, a_top2, n)
            at(p + OW, a_wT, n)
            o = CH * n
            for ex in range(1, EXPERTS):
                at(o + START + 4 * ex - WB, f_wb, n, ex)
            at(o + START + CH + LAG + FN, f_fin, n)

        stages = {"h": (f_hi, HL), "u": (f_up, 0), "g": (f_gelu, 0), "l": (f_lo, LL), "d": (f_down, LAG)}
        for slot in range(min(plan), START + CH * NG + LAG + FN + 1):
            S["slot"] = slot
            for step in ORDER:
                if step == "a":
                    for fn, args in plan.get(slot, []):
                        fn(*args)
                else:
                    fn, lag = stages[step]
                    k = slot - START - lag
                    if 0 <= k < CH * NG:
                        fn(k // CH, k % CH)

        block = ctx.enter_context(nc.Block())

        @block.sync
        def _(e):
            Q.play("sync", e)
            for p in range(2):
                e.wait_ge(Q.sems[f"d_out{p}"], Q.count[f"d_out{p}"])
                e.wait_ge(Q.sems[f"d_wd{p}"], Q.count[f"d_wd{p}"])
                e.wait_ge(Q.sems[f"d_nw{p}"], Q.count[f"d_nw{p}"])
            for name in ("d_Qw", "d_Kw", "d_km"):
                e.wait_ge(Q.sems[name], Q.count[name])

        @block.scalar
        def _(e):
            Q.play("scalar", e)

        @block.vector
        def _(e):
            Q.play("vector", e)

        @block.gpsimd
        def _(e):
            Q.play("gpsimd", e)

        @block.tensor
        def _(e):
            Q.play("tensor", e)


def kernel(**inputs):
    import concourse.bacc as bacc
    from concourse.bass_utils import run_bass_kernel_spmd

    def a(name):
        return np.asarray(inputs[name])

    def c(v):
        return np.ascontiguousarray(v)

    mask = c(a("mask_BxS2_bf0")).view(np.uint8)
    arrays = {
        "x": c(a("x")),
        "ctxT": c(a("ctx_1024").transpose(2, 0, 1).reshape(D, NB * LK)),
        "mask": mask.view(np.int32),
        "maskT": c(mask.T).view(np.int32),
        "wqT": c(a("L0_xattn_wq").T),
        "wkT": c(a("L0_xattn_wk").T),
        "wvT": c(a("L0_xattn_wv").T),
        "woT": c(a("L0_xattn_wo").T),
        "bqT": c(a("L0_xattn_bq").reshape(128, 1)),
        "bkT": c(a("L0_xattn_bk").reshape(128, 1)),
        "bv": c(a("L0_xattn_bv")),
        "bo": c(a("L0_xattn_bo")),
        "gate_w": c(a("L0_ffn_gate_w")),
        "gbias": c(a("L0_ffn_bias").reshape(8, 1)),
        "up_w": c(a("L0_ffn_up_w")),
        "up_bT": c(a("L0_ffn_up_b").reshape(8, 4, 128).transpose(2, 0, 1).reshape(128, 32)),
        "down_w": c(a("L0_ffn_down_w")),
        "down_bT": c(a("L0_ffn_down_b").T),
        "sw_up": c(a("L0_ffn_sw_up")),
        "sb_upT": c(a("L0_ffn_sb_up").reshape(4, 128).T),
        "sw_down": c(a("L0_ffn_sw_down")),
        "sb_downT": c(a("L0_ffn_sb_down").reshape(128, 1)),
        "consts": constants(),
    }
    nc = bacc.Bacc("TRN2", target_bir_lowering=False, num_devices=1)
    feeds, args = {}, []
    for name, v in arrays.items():
        feeds[f"in_{name}"] = v
        args.append(nc.dram_tensor(f"in_{name}", v.shape, mybir.dt.from_np(v.dtype), kind="ExternalInput").ap())
    args.append(nc.dram_tensor("out_0", (NB, LQ, D), F32, kind="ExternalOutput").ap())
    xattn_moe_kernel(nc, *args)
    r = run_bass_kernel_spmd(nc, [feeds], core_ids=[0])
    return r.results[0]["out_0"]
```
